# Optimizing a Trainium2 kernel written in Bass

```python
import numpy as np
import jax
import jax.numpy as jnp

def _softmax(x, axis=-1):
    return jax.nn.softmax(x, axis=axis)

def _gelu(x):
    return jax.nn.gelu(x, approximate=True)

def _silu(x):
    return jax.nn.silu(x)

def _sigmoid(x):
    return jax.nn.sigmoid(x)

def _layernorm(x, axis=-1, eps=1e-05):
    m = jnp.mean(x, axis=axis, keepdims=True)
    v = jnp.var(x, axis=axis, keepdims=True)
    return (x - m) / jnp.sqrt(v + eps)

def _scatter_add(tgt, idx, src, axis=0):
    return tgt.at[idx].add(src)

def _segment_sum(src, seg, n):
    return jax.ops.segment_sum(src, seg, n)
kernel_name = 'mk_gnn_resnorm_d4_gnn_r32_0b03c5'

def setup_inputs(seed: int=0):
    np.random.seed(seed)
    _w = jnp.asarray

    def _rec_inputs():
        import jax
        import jax.numpy as jnp
        _gk = jax.random.key(seed)
        x = -0.0009044 + 1 * jax.random.normal(jax.random.fold_in(_gk, 1), (3125, 16), jnp.float32)
        src = jax.random.randint(jax.random.fold_in(_gk, 2), (100000,), 0, 3125, jnp.int32)
        dst = jnp.minimum((3125 * jax.random.uniform(jax.random.fold_in(_gk, 3), (100000,)) ** 2.0).astype(jnp.int32), 99999)
        _o = jnp.argsort(dst, stable=True)
        src = src[_o]
        dst = dst[_o]
        edge_attr_16 = 0.000189758 + 1.00013 * jax.random.normal(jax.random.fold_in(_gk, 11), (100000, 16), jnp.float32)
        edge_attr_2 = -0.000107899 + 1.00008 * jax.random.normal(jax.random.fold_in(_gk, 12), (100000, 2), jnp.float32)
        edge_attr_3 = -1.09012e-05 + 0.99985 * jax.random.normal(jax.random.fold_in(_gk, 13), (100000, 3), jnp.float32)
        edge_attr_48 = -3.69585e-06 + 0.999911 * jax.random.normal(jax.random.fold_in(_gk, 14), (100000, 48), jnp.float32)
        return (x, src, dst, edge_attr_16, edge_attr_2, edge_attr_3, edge_attr_48)
    x, src, dst, edge_attr_16, edge_attr_2, edge_attr_3, edge_attr_48 = _rec_inputs()

    def _L0_gnn_setup():
        import jax, jax.numpy as jnp
        import numpy as np
        N_NODES = 3125
        N_EDGES = 100000
        D_FEAT = 16
        key = jax.random.key(seed)
        k1, k2, k3 = jax.random.split(key, 3)
        x = jax.random.normal(k1, (N_NODES, D_FEAT), dtype=jnp.float32)
        edge_index = jax.random.randint(k2, (2, N_EDGES), 0, N_NODES, dtype=jnp.int64)
        edge_attr = jax.random.normal(k3, (N_EDGES, D_FEAT), dtype=jnp.float32)
        return {'x': x, 'edge_index': edge_index, 'edge_attr': edge_attr}
    _L0_gnn_all = _L0_gnn_setup()
    _L0_gnn_in = {k: v for k, v in _L0_gnn_all.items() if k in ()}
    del _L0_gnn_all

    def _L1_gnn_setup():
        import jax, jax.numpy as jnp
        import numpy as np
        NS, NV = (16, 4)
        EPS = 1e-05
        N_NODES, N_EDGES = (1250, 12500)

        def _bn_scalar(x, g, b):
            m = x.mean(0)
            v = ((x - m) ** 2).mean(0)
            return (x - m) / jnp.sqrt(v + EPS) * g + b

        def _seg_mean(x, idx, n):
            s = jax.ops.segment_sum(x, idx, num_segments=n)
            c = jax.ops.segment_sum(jnp.ones((idx.shape[0],), x.dtype), idx, num_segments=n)
            return s / jnp.maximum(c, 1.0)[:, None]

        def _edge_weights(edge_attr, w1, b1, w2, b2):
            h = jax.nn.relu(edge_attr @ w1 + b1)
            return h @ w2 + b2

        def _forward(node_attr, edge_attr, edge_vec, fc0_w1, fc0_b1, fc0_w2, fc0_b2, fc1_w1, fc1_b1, fc1_w2, fc1_b2, bn0_gs, bn0_bs, bn0_gv, bn1_gs, bn1_bs, edge_index):
            N = node_attr.shape[0]
            E = edge_attr.shape[0]
            src, dst = (edge_index[0], edge_index[1])
            rhat = edge_vec / (jnp.linalg.norm(edge_vec, axis=-1, keepdims=True) + 1e-12)
            sh1 = rhat * float(np.sqrt(3.0))
            w = _edge_weights(edge_attr, fc0_w1, fc0_b1, fc0_w2, fc0_b2)
            wa = w[:, :NS * NS].reshape(E, NS, NS)
            wb = w[:, NS * NS:].reshape(E, NS, NV)
            x = node_attr[dst]
            inv = float(1.0 / np.sqrt(NS))
            msg_s = jnp.einsum('ei,eij->ej', x, wa) * inv
            msg_v = jnp.einsum('ei,eij,ec->ejc', x, wb, sh1) * inv
            msg = jnp.concatenate([msg_s, msg_v.reshape(E, NV * 3)], axis=-1)
            out = _seg_mean(msg, src, N)
            s0 = _bn_scalar(out[:, :NS], bn0_gs, bn0_bs)
            v0 = out[:, NS:].reshape(N, NV, 3)
            vn = jnp.sqrt((v0 ** 2).mean(axis=(0, 2)) + EPS)
            v0 = v0 / vn[None, :, None] * bn0_gv[None, :, None]
            w = _edge_weights(edge_attr, fc1_w1, fc1_b1, fc1_w2, fc1_b2)
            wa = w[:, :NS * NS].reshape(E, NS, NS)
            wb = w[:, NS * NS:].reshape(E, NV, NS)
            s = s0[dst]
            v = v0[dst]
            path_a = jnp.einsum('ei,eij->ej', s, wa)
            path_b = jnp.einsum('eic,ec,eij->ej', v, sh1, wb) * float(1.0 / np.sqrt(3.0))
            msg = (path_a + path_b) * float(1.0 / np.sqrt(NS + NV))
            node1 = _seg_mean(msg, src, N)
            return _bn_scalar(node1, bn1_gs, bn1_bs)
        key = jax.random.key(seed)
        ks = jax.random.split(key, 8)
        d = 3 * NS
        wn = NS * NS + NS * NV
        g = lambda k, shape, sc: jax.random.normal(k, shape, jnp.float32) * sc
        return {'node_attr': g(ks[0], (N_NODES, NS), 1.0), 'edge_attr': g(ks[1], (N_EDGES, d), 1.0), 'edge_vec': g(ks[2], (N_EDGES, 3), 1.0), 'fc0_w1': g(ks[3], (d, d), d ** (-0.5)), 'fc0_b1': jnp.zeros((d,), jnp.float32), 'fc0_w2': g(ks[4], (d, wn), d ** (-0.5)), 'fc0_b2': jnp.zeros((wn,), jnp.float32), 'fc1_w1': g(ks[5], (d, d), d ** (-0.5)), 'fc1_b1': jnp.zeros((d,), jnp.float32), 'fc1_w2': g(ks[6], (d, wn), d ** (-0.5)), 'fc1_b2': jnp.zeros((wn,), jnp.float32), 'bn0_gs': jnp.ones((NS,), jnp.float32), 'bn0_bs': jnp.zeros((NS,), jnp.float32), 'bn0_gv': jnp.ones((NV,), jnp.float32), 'bn1_gs': jnp.ones((NS,), jnp.float32), 'bn1_bs': jnp.zeros((NS,), jnp.float32), 'edge_index': jax.random.randint(ks[7], (2, N_EDGES), 0, N_NODES)}
    _L1_gnn_all = _L1_gnn_setup()
    _L1_gnn_in = {k: v for k, v in _L1_gnn_all.items() if k in ('fc0_w1', 'fc0_b1', 'fc0_w2', 'fc0_b2', 'fc1_w1', 'fc1_b1', 'fc1_w2', 'fc1_b2', 'bn0_gs', 'bn0_bs', 'bn0_gv', 'bn1_gs', 'bn1_bs')}
    del _L1_gnn_all

    def _L2_gnn_setup():
        import jax, jax.numpy as jnp
        import numpy as np
        BN_EPS = 1e-05
        LRELU_SLOPE = 0.01
        key = jax.random.key(seed)
        ks = jax.random.split(key, 8)
        N, E, IN, OUT, EF = (50000, 50000, 16, 16, 2)
        return {'v': jax.random.normal(ks[0], (N, IN), jnp.float32), 'e': jax.random.normal(ks[1], (E, EF), jnp.float32), 'edge_index': jax.random.randint(ks[2], (2, E), 0, N, jnp.int64), 'W_enet': jax.random.normal(ks[3], (EF, IN * OUT), jnp.float32) * 0.1, 'b_enet': jax.random.normal(ks[4], (IN * OUT,), jnp.float32) * 0.1, 'W_root': jax.random.normal(ks[5], (IN, OUT), jnp.float32) * 0.1, 'bias': jax.random.normal(ks[6], (OUT,), jnp.float32) * 0.1, 'gamma': jnp.ones((OUT,), jnp.float32), 'beta': jnp.zeros((OUT,), jnp.float32)}
    _L2_gnn_all = _L2_gnn_setup()
    _L2_gnn_in = {k: v for k, v in _L2_gnn_all.items() if k in ('W_enet', 'b_enet', 'W_root', 'bias', 'gamma', 'beta')}
    del _L2_gnn_all

    def _L3_gnn_setup():
        import jax, jax.numpy as jnp
        import numpy as np
        key = jax.random.key(seed)
        k1, k2, k3, k4 = jax.random.split(key, 4)
        N, E, D = (3125, 100000, 16)
        x = jax.random.normal(k1, (N, D), dtype=jnp.float32)
        edge_index = jax.random.randint(k2, (2, E), 0, N, dtype=jnp.int64)
        s = 1.0 / np.sqrt(D)
        W1 = jax.random.normal(k3, (D, 16), dtype=jnp.float32) * s
        b1 = jnp.zeros((16,), dtype=jnp.float32)
        W2 = jax.random.normal(k4, (16, 16), dtype=jnp.float32) * s
        b2 = jnp.zeros((16,), dtype=jnp.float32)
        return {'x': x, 'edge_index': edge_index, 'W1': W1, 'b1': b1, 'W2': W2, 'b2': b2}
    _L3_gnn_all = _L3_gnn_setup()
    _L3_gnn_in = {k: v for k, v in _L3_gnn_all.items() if k in ('W1', 'b1', 'W2', 'b2')}
    del _L3_gnn_all
    return {'x': x, 'src': src, 'dst': dst, 'edge_attr_16': edge_attr_16, 'edge_attr_2': edge_attr_2, 'edge_attr_3': edge_attr_3, 'edge_attr_48': edge_attr_48, 'L1_gnn_fc0_w1': _L1_gnn_in['fc0_w1'], 'L1_gnn_fc0_b1': _L1_gnn_in['fc0_b1'], 'L1_gnn_fc0_w2': _L1_gnn_in['fc0_w2'], 'L1_gnn_fc0_b2': _L1_gnn_in['fc0_b2'], 'L1_gnn_fc1_w1': _L1_gnn_in['fc1_w1'], 'L1_gnn_fc1_b1': _L1_gnn_in['fc1_b1'], 'L1_gnn_fc1_w2': _L1_gnn_in['fc1_w2'], 'L1_gnn_fc1_b2': _L1_gnn_in['fc1_b2'], 'L1_gnn_bn0_gs': _L1_gnn_in['bn0_gs'], 'L1_gnn_bn0_bs': _L1_gnn_in['bn0_bs'], 'L1_gnn_bn0_gv': _L1_gnn_in['bn0_gv'], 'L1_gnn_bn1_gs': _L1_gnn_in['bn1_gs'], 'L1_gnn_bn1_bs': _L1_gnn_in['bn1_bs'], 'L2_gnn_W_enet': _L2_gnn_in['W_enet'], 'L2_gnn_b_enet': _L2_gnn_in['b_enet'], 'L2_gnn_W_root': _L2_gnn_in['W_root'], 'L2_gnn_bias': _L2_gnn_in['bias'], 'L2_gnn_gamma': _L2_gnn_in['gamma'], 'L2_gnn_beta': _L2_gnn_in['beta'], 'L3_gnn_W1': _L3_gnn_in['W1'], 'L3_gnn_b1': _L3_gnn_in['b1'], 'L3_gnn_W2': _L3_gnn_in['W2'], 'L3_gnn_b2': _L3_gnn_in['b2']}

def reference(x, src, dst, edge_attr_16, edge_attr_2, edge_attr_3, edge_attr_48, L1_gnn_fc0_w1, L1_gnn_fc0_b1, L1_gnn_fc0_w2, L1_gnn_fc0_b2, L1_gnn_fc1_w1, L1_gnn_fc1_b1, L1_gnn_fc1_w2, L1_gnn_fc1_b2, L1_gnn_bn0_gs, L1_gnn_bn0_bs, L1_gnn_bn0_gv, L1_gnn_bn1_gs, L1_gnn_bn1_bs, L2_gnn_W_enet, L2_gnn_b_enet, L2_gnn_W_root, L2_gnn_bias, L2_gnn_gamma, L2_gnn_beta, L3_gnn_W1, L3_gnn_b1, L3_gnn_W2, L3_gnn_b2):
    import jax
    import jax.numpy as jnp

    def _L0_gnn_ref(x, edge_index, edge_attr):
        import jax, jax.numpy as jnp
        import numpy as np
        N_NODES = 3125
        N_EDGES = 100000
        D_FEAT = 16
        nb_node = x.shape[0]
        dst = edge_index[1]
        sums = jax.ops.segment_sum(edge_attr, dst, num_segments=nb_node)
        counts = jax.ops.segment_sum(jnp.ones((edge_attr.shape[0],), dtype=edge_attr.dtype), dst, num_segments=nb_node)
        denom = jnp.where(counts > 0, counts, jnp.ones_like(counts))
        return sums / denom[:, None]

    def _L1_gnn_ref(node_attr, edge_attr, edge_vec, fc0_w1, fc0_b1, fc0_w2, fc0_b2, fc1_w1, fc1_b1, fc1_w2, fc1_b2, bn0_gs, bn0_bs, bn0_gv, bn1_gs, bn1_bs, edge_index):
        import jax, jax.numpy as jnp
        import numpy as np
        NS, NV = (16, 4)
        EPS = 1e-05
        N_NODES, N_EDGES = (1250, 12500)

        def _bn_scalar(x, g, b):
            m = x.mean(0)
            v = ((x - m) ** 2).mean(0)
            return (x - m) / jnp.sqrt(v + EPS) * g + b

        def _seg_mean(x, idx, n):
            s = jax.ops.segment_sum(x, idx, num_segments=n)
            c = jax.ops.segment_sum(jnp.ones((idx.shape[0],), x.dtype), idx, num_segments=n)
            return s / jnp.maximum(c, 1.0)[:, None]

        def _edge_weights(edge_attr, w1, b1, w2, b2):
            h = jax.nn.relu(edge_attr @ w1 + b1)
            return h @ w2 + b2

        def _forward(node_attr, edge_attr, edge_vec, fc0_w1, fc0_b1, fc0_w2, fc0_b2, fc1_w1, fc1_b1, fc1_w2, fc1_b2, bn0_gs, bn0_bs, bn0_gv, bn1_gs, bn1_bs, edge_index):
            N = node_attr.shape[0]
            E = edge_attr.shape[0]
            src, dst = (edge_index[0], edge_index[1])
            rhat = edge_vec / (jnp.linalg.norm(edge_vec, axis=-1, keepdims=True) + 1e-12)
            sh1 = rhat * float(np.sqrt(3.0))
            w = _edge_weights(edge_attr, fc0_w1, fc0_b1, fc0_w2, fc0_b2)
            wa = w[:, :NS * NS].reshape(E, NS, NS)
            wb = w[:, NS * NS:].reshape(E, NS, NV)
            x = node_attr[dst]
            inv = float(1.0 / np.sqrt(NS))
            msg_s = jnp.einsum('ei,eij->ej', x, wa) * inv
            msg_v = jnp.einsum('ei,eij,ec->ejc', x, wb, sh1) * inv
            msg = jnp.concatenate([msg_s, msg_v.reshape(E, NV * 3)], axis=-1)
            out = _seg_mean(msg, src, N)
            s0 = _bn_scalar(out[:, :NS], bn0_gs, bn0_bs)
            v0 = out[:, NS:].reshape(N, NV, 3)
            vn = jnp.sqrt((v0 ** 2).mean(axis=(0, 2)) + EPS)
            v0 = v0 / vn[None, :, None] * bn0_gv[None, :, None]
            w = _edge_weights(edge_attr, fc1_w1, fc1_b1, fc1_w2, fc1_b2)
            wa = w[:, :NS * NS].reshape(E, NS, NS)
            wb = w[:, NS * NS:].reshape(E, NV, NS)
            s = s0[dst]
            v = v0[dst]
            path_a = jnp.einsum('ei,eij->ej', s, wa)
            path_b = jnp.einsum('eic,ec,eij->ej', v, sh1, wb) * float(1.0 / np.sqrt(3.0))
            msg = (path_a + path_b) * float(1.0 / np.sqrt(NS + NV))
            node1 = _seg_mean(msg, src, N)
            return _bn_scalar(node1, bn1_gs, bn1_bs)
        return _forward(node_attr, edge_attr, edge_vec, fc0_w1, fc0_b1, fc0_w2, fc0_b2, fc1_w1, fc1_b1, fc1_w2, fc1_b2, bn0_gs, bn0_bs, bn0_gv, bn1_gs, bn1_bs, edge_index)

    def _L2_gnn_ref(v, e, edge_index, W_enet, b_enet, W_root, bias, gamma, beta):
        import jax, jax.numpy as jnp
        import numpy as np
        BN_EPS = 1e-05
        LRELU_SLOPE = 0.01
        N, in_dim = v.shape
        out_dim = W_root.shape[1]
        src, tgt = (edge_index[0], edge_index[1])
        W_e = (e @ W_enet + b_enet).reshape(-1, in_dim, out_dim)
        msg = jnp.einsum('ei,eio->eo', v[src], W_e)
        agg_sum = jax.ops.segment_sum(msg, tgt, num_segments=N)
        cnt = jax.ops.segment_sum(jnp.ones((msg.shape[0],), v.dtype), tgt, num_segments=N)
        agg = agg_sum / jnp.maximum(cnt, 1.0)[:, None]
        h = agg + v @ W_root + bias
        mean = jnp.mean(h, axis=0)
        var = jnp.mean((h - mean) ** 2, axis=0)
        h = (h - mean) * jax.lax.rsqrt(var + BN_EPS) * gamma + beta
        h = jnp.where(h >= 0, h, LRELU_SLOPE * h)
        return h + v

    def _L3_gnn_ref(x, edge_index, W1, b1, W2, b2):
        import jax, jax.numpy as jnp
        import numpy as np
        N = x.shape[0]
        loop = jnp.arange(N, dtype=edge_index.dtype)
        row = jnp.concatenate([edge_index[0], loop])
        col = jnp.concatenate([edge_index[1], loop])
        deg = jax.ops.segment_sum(jnp.ones_like(col, dtype=x.dtype), col, num_segments=N)
        dinv = jnp.where(deg > 0, jax.lax.rsqrt(deg), 0.0)
        norm = dinv[row] * dinv[col]

        def gcn_conv(h, W, b):
            hw = h @ W
            msg = hw[row] * norm[:, None]
            agg = jax.ops.segment_sum(msg, col, num_segments=N)
            return agg + b
        h = jnp.tanh(gcn_conv(x, W1, b1))
        h = jnp.tanh(gcn_conv(h, W2, b2))
        return h
    edge_index = jnp.stack([src, dst])
    x = _layernorm(x + _L0_gnn_ref(x, edge_index, edge_attr_16), axis=-1)
    x = _layernorm(x + _L1_gnn_ref(x, edge_attr_48, edge_attr_3, L1_gnn_fc0_w1, L1_gnn_fc0_b1, L1_gnn_fc0_w2, L1_gnn_fc0_b2, L1_gnn_fc1_w1, L1_gnn_fc1_b1, L1_gnn_fc1_w2, L1_gnn_fc1_b2, L1_gnn_bn0_gs, L1_gnn_bn0_bs, L1_gnn_bn0_gv, L1_gnn_bn1_gs, L1_gnn_bn1_bs, edge_index), axis=-1)
    x = _layernorm(x + _L2_gnn_ref(x, edge_attr_2, edge_index, L2_gnn_W_enet, L2_gnn_b_enet, L2_gnn_W_root, L2_gnn_bias, L2_gnn_gamma, L2_gnn_beta), axis=-1)
    x = _layernorm(x + _L3_gnn_ref(x, edge_index, L3_gnn_W1, L3_gnn_b1, L3_gnn_W2, L3_gnn_b2), axis=-1)
    return x

_drawn_inputs = setup_inputs


def setup_inputs(seed=0):
    import zlib

    import numpy as np

    out = dict(_drawn_inputs(seed))
    spreads = {'L1_gnn_fc0_b1': (0.0, 0.1),
     'L1_gnn_fc0_b2': (0.0, 0.1),
     'L1_gnn_fc1_b1': (0.0, 0.1),
     'L1_gnn_fc1_b2': (0.0, 0.1),
     'L1_gnn_bn0_gs': (1.0, 0.2),
     'L1_gnn_bn0_bs': (0.0, 0.1),
     'L1_gnn_bn0_gv': (1.0, 0.2),
     'L1_gnn_bn1_gs': (1.0, 0.2),
     'L1_gnn_bn1_bs': (0.0, 0.1),
     'L2_gnn_gamma': (1.0, 0.2),
     'L2_gnn_beta': (0.0, 0.1),
     'L3_gnn_b1': (0.0, 0.1),
     'L3_gnn_b2': (0.0, 0.1)}
    factors = {}
    for name, (base, spread) in spreads.items():
        noise = np.random.default_rng([zlib.crc32(name.encode()), seed]).standard_normal(out[name].shape)
        drawn = base * np.exp(spread * noise) if base else spread * noise
        out[name] = jnp.asarray(drawn.astype(out[name].dtype))
    for name, factor in factors.items():
        out[name] = (out[name] * factor).astype(out[name].dtype)
    return out
```

```python
from contextlib import ExitStack

import concourse.bass as bass
from concourse import mybir

ALU = mybir.AluOpType
ACT = mybir.ActivationFunctionType
AX = mybir.AxisListType
F32 = mybir.dt.float32
BF16 = mybir.dt.bfloat16
I32 = mybir.dt.int32
RMAX = bass.bass_isa.ReduceOp.max

P = 128
N = 3125
E = 100000
D = 16
NB = -(-N // P)
NP_ = NB * P
T = 8
SUP = T * P
NSUP = 98
EP = NSUP * SUP
PAIRS = NSUP // 2
EK = 48
NV = 4
MJ = D + NV
MF = D + 3 * NV
EPS = 1e-5
DUMP = NP_ - 1
BIAS = NB - 1
assert NSUP % 2 == 0 and EP >= E and NP_ > N


def repeat(ap, axis, n):
    wide = ap.unsqueeze(axis)
    shape = list(wide.shape)
    shape[axis] = n
    return wide.broadcast_to(shape)


def build(nc, a):
    with ExitStack() as ctx:
        def sb(name, shape, dt=F32):
            return ctx.enter_context(nc.sbuf_tensor(name, shape, dt))

        def sem(name):
            return ctx.enter_context(nc.semaphore(name))

        dst_i = sb("dst_i", [P, NSUP, T], I32)
        dst_f = sb("dst_f", [P, NSUP, T])
        src_i = sb("src_i", [P, NSUP, T], I32)
        src_t = sb("src_t", [P, NSUP, T], I32)
        src_lo = sb("src_lo", [P, NSUP, T])
        src_hi = sb("src_hi", [P, NSUP, T])
        rhat = sb("rhat", [P, NSUP, T, 3])
        rn = sb("rn", [P, NSUP, T])
        ea2 = sb("ea2", [P, NSUP, T, 2])
        big = sb("big", [P, 2, T, NB, MF])
        rsq = big[:, 0, :, :, :].rearrange("p t h f -> p (t h f)")[:, 0:NSUP * T * 3]
        iota_i = sb("iota_i", [P, NP_], I32)
        iota_f = sb("iota_f", [P, NP_])
        pid_i = sb("pid_i", [P, 1], I32)
        pid_f = sb("pid_f", [P, 1])
        ident = sb("ident", [P, P])
        ones = sb("ones", [P, P])
        zeros = sb("zeros", [P, 512], BF16)
        mask = sb("mask", [P, NB])
        node_id = sb("node_id", [P, NB])
        ext = sb("ext", [P, 2, NSUP])
        extp = sb("extp", [P, 2, NSUP])
        ext_i = sb("ext_i", [P, 2, NSUP], I32)
        blk_i = sb("blk_i", [P, 2, NSUP], I32)
        blk = sb("blk", [P, 2, NSUP])
        cnt_w = sb("cnt_w", [P, NSUP])
        cum_w = sb("cum_w", [P, NSUP])
        win_f = sb("win_f", [P, NSUP, 4])
        win = sb("win", [P, NSUP, 4], I32)
        neg_dst = sb("neg_dst", [P, NSUP, T])

        ea16 = sb("ea16", [P, 2, T, D])
        vals = sb("vals", [P, 2, T, D + 1])
        onehot = sb("onehot", [P, 2, T // 2, P])
        oh_lo = sb("oh_lo", [P, 2, T, P])
        oh_hi = sb("oh_hi", [P, 2, T, NB])
        eat = sb("eat", [EK, 2, SUP])
        ht = sb("ht", [EK + 1, 2, SUP])
        idx = sb("idx", [P, 2, T], I32)
        gb = sb("gb", [P, 2, T, 32])
        vprod = sb("vprod", [P, T, NV, 3])
        prod = sb("prod", [P, 2, 2, MJ * D])
        msg = sb("msg", [P, 2, T, 32])
        v48 = sb("v48", [P, 2, T, 3 * D])
        w1 = [sb(f"w1_{l}", [EK, P]) for l in range(2)]
        b1 = [sb(f"b1_{l}", [EK, 1]) for l in range(2)]
        w2 = [sb(f"w2_{l}", [EK + 1, MJ * D]) for l in range(2)]
        par = sb("par", [P, 9, D])
        GS0, BS0, GV0, GS1, BS1, B2, GA, BE, C1 = range(9)
        c2 = sb("c2", [P, D])
        wst = sb("wst", [4 * D, D])
        gw1 = sb("gw1", [D, D])
        gw2 = sb("gw2", [D, D])

        x = sb("x", [P, NB, D])
        acc = sb("acc", [P, NB, 64])
        t1 = sb("t1", [P, NB, 32])
        t2 = sb("t2", [P, NB, 32])
        r1 = sb("r1", [P, NB])
        rcd = sb("rcd", [P, NB])
        rcs = sb("rcs", [P, NB])
        dinv = sb("dinv", [P, NB])
        tab = sb("tab", [P, NB, 32])
        hh = sb("hh", [P, NB, D])
        stat = sb("stat", [P, 32])
        sm = sb("sm", [P, 32])
        sv = sb("sv", [P, 32])
        r1_root = sb("r1_root", [P, NB])
        r1_t = sb("r1_t", [P, NB])
        sv_root = sb("sv_root", [P, D])
        sv_t = sb("sv_t", [P, D])
        rn_root = big[:, 1, :, :, :].rearrange("p t h f -> p (t h f)")[:, 0:NSUP * T]
        rn_t = big[:, 1, :, :, :].rearrange("p t h f -> p (t h f)")[:, NSUP * T:2 * NSUP * T]
        xt = sb("xt", [4 * D, NB, P])

        ps = ctx.enter_context(nc.psum_tensor("ps", [P, 8, 512], F32))
        psf = ps[:, :, :].rearrange("p b n -> p (b n)")
        TBANK = [0, 1, 2, 3, 4, 6, 7]

        s_par = sem("s_par")
        s_idx0 = sem("s_idx0")
        s_x = sem("s_x")
        s_iota = sem("s_iota")
        s_dve = sem("s_dve")
        s_ext = sem("s_ext")
        s_extp = sem("s_extp")
        s_setup = sem("s_setup")
        s_node = sem("s_node")
        s_tab = sem("s_tab")
        s_tabr = sem("s_tabr")
        s_str = sem("s_str")
        s_sts = sem("s_sts")
        s_nmi = sem("s_nmi")
        s_nmt = sem("s_nmt")
        s_nmc = sem("s_nmc")
        s_nmo = sem("s_nmo")
        s_accd = sem("s_accd")
        s_zero = sem("s_zero")
        s_th = sem("s_th")
        s_sqi = sem("s_sqi")
        s_sqo = sem("s_sqo")
        s_thi = sem("s_thi")
        s_fin = sem("s_fin")
        s_out = sem("s_out")

        oh_ready = [[sem(f"oh_ready{p}_{h}") for h in range(2)] for p in range(4)]
        oh_used = [[sem(f"oh_used{p}_{h}") for h in range(2)] for p in range(4)]
        row_used = [sem(f"row_used{p}") for p in range(4)]
        ea_in = [sem(f"ea_in{b}") for b in range(2)]
        ea_cp = sem("ea_cp")
        sc_oh = sem("sc_oh")
        idx_in = [[sem(f"idx_in{p}_{b}") for b in range(2)] for p in range(5)]
        g_in = [[sem(f"g_in{p}_{b}") for b in range(2)] for p in range(5)]
        g_used = [sem(f"g_used{p}") for p in range(5)]
        eat_in = [[sem(f"eat_in{l}_{b}") for b in range(2)] for l in range(2)]
        h_mm = [sem(f"h_mm{l}") for l in range(2)]
        h_act = [sem(f"h_act{l}") for l in range(2)]
        w_mm = [sem(f"w_mm{l}") for l in range(2)]
        p_done = [sem(f"p_done{l}") for l in range(2)]
        r_done = [sem(f"r_done{l}") for l in range(2)]
        q_done = [sem(f"q_done{l}") for l in range(2)]
        o_done = [sem(f"o_done{l}") for l in range(2)]
        l_done = [sem(f"l_done{l}") for l in range(2)]
        sc_mm = [sem(f"sc_mm{l}") for l in range(2)]
        v_done = sem("v_done")

        tabs = [nc.dram_tensor(f"table{p}", (NP_, w), F32, kind="Internal").ap()
                for p, w in enumerate([D, MF, D, D, D])]
        tabw = [D, MF, D, D, D]

        block = ctx.enter_context(nc.Block())

        e3 = a["edge_attr_3"].rearrange("(s p t) c -> p s (t c)", p=P, t=T)
        e2 = a["edge_attr_2"].rearrange("(s p t) c -> p s (t c)", p=P, t=T)
        e16 = a["edge_attr_16"].rearrange("(s p t) c -> s p (t c)", p=P, t=T)
        srcv = a["src"].rearrange("(s p t) -> p s t", p=P, t=T)
        dstv = a["dst"].rearrange("(s p t) -> p s t", p=P, t=T)
        gidx = [a["dst"], a["dst"], a["src"], a["src"], a["src"]]
        gidxv = [g.rearrange("(s p t) -> s p t", p=P, t=T) for g in gidx]
        WIN = {0: 0, 2: 1, 3: 2, 4: 3}

        @block.sync
        def _(sp):
            sp.dma_start(dst_i[:, :, :], dstv).then_inc(s_idx0, 16)
            sp.dma_start(src_i[:, :, :], srcv).then_inc(s_idx0, 16)
            sp.dma_start(rhat[:, :, :, :].rearrange("p s t c -> p s (t c)"), e3).then_inc(s_idx0, 16)
            sp.dma_start(ea2[:, :, :, :].rearrange("p s t c -> p s (t c)"), e2).then_inc(s_idx0, 16)
            sp.dma_start(x[:, :, :], a["x"].rearrange("(q p) f -> p q f", p=P)).then_inc(s_x, 16)
            for l in range(2):
                sp.dma_start(w1[l][:, :], a[f"w1_{l}"]).then_inc(s_par, 16)
                sp.dma_start(b1[l][:, :], a[f"b1_{l}"].rearrange("(k o) -> k o", o=1)).then_inc(s_par, 16)
                sp.dma_start(w2[l][:, :], a[f"w2_{l}"]).then_inc(s_par, 16)
            sp.dma_start(wst[0:2 * D, :], a["w_enet"]).then_inc(s_par, 16)
            sp.dma_start(wst[2 * D:3 * D, :], a["b_enet"]).then_inc(s_par, 16)
            sp.dma_start(wst[3 * D:4 * D, :], a["w_root"]).then_inc(s_par, 16)
            sp.dma_start(gw1[:, :], a["gw1"]).then_inc(s_par, 16)
            sp.dma_start(gw2[:, :], a["gw2"]).then_inc(s_par, 16)
            for i, n in enumerate(["gs0", "bs0", "gv0", "gs1", "bs1", "bias", "gamma", "beta", "gb1"]):
                k = a[n].shape[0]
                sp.dma_start(par[:, i, 0:k], a[n].rearrange("(o k) -> o k", o=1).broadcast_to([P, k])).then_inc(s_par, 16)
            sp.dma_start(c2[:, :], a["gb2"].rearrange("(o k) -> o k", o=1).broadcast_to([P, D])).then_inc(s_par, 16)

            with sp.Fori(0, PAIRS) as i:
                for b in range(2):
                    sp.wait_ge(ea_cp, i * 2 + b + 1)
                    sp.dma_start(ea16[:, b, :, :].rearrange("p t f -> p (t f)"),
                                 e16[bass.ds(i * 2 + b, 1), :, :].rearrange("o p f -> p (o f)")).then_inc(ea_in[b], 16)

            def store_table(p):
                sp.wait_ge(s_tabr, p + 1)
                sp.dma_start(tabs[p].rearrange("(q p) f -> p q f", p=P), tab[:, :, 0:tabw[p]]).then_inc(s_tab, 16)

            def load_idx(p, b, i):
                sp.dma_start(idx[:, b, :], gidxv[p][bass.ds(i * 2 + b, 1), :, :].rearrange("o p t -> p (o t)")).then_inc(idx_in[p][b], 16)

            for l in range(2):
                store_table(l)
                with sp.Fori(0, PAIRS) as i:
                    for b in range(2):
                        sp.wait_ge(h_mm[l], (i * 2 + b) * 2 + 1)
                        sp.dma_start(eat[:, b, :], a["eat"][bass.ds(i * 2 + b, 1), :, :].rearrange("o k n -> k (o n)")).then_inc(eat_in[l][b], 16)
                        sp.wait_ge(g_used[l], i * 2 + b + 1)
                        load_idx(l, b, i)
            for p in range(2, 5):
                store_table(p)
                with sp.Fori(0, PAIRS) as i:
                    for b in range(2):
                        sp.wait_ge(g_used[p], i * 2 + b + 1)
                        load_idx(p, b, i)
            sp.wait_ge(s_fin, 1)
            full = N // P
            sp.dma_start(a["out"][0:full * P, :].rearrange("(q p) f -> p q f", p=P), x[:, 0:full, :]).then_inc(s_out, 16)
            sp.dma_start(a["out"][full * P:N, :], x[0:N - full * P, full, :]).then_inc(s_out, 16)
            sp.wait_ge(s_out, 32)
            sp.wait_ge(s_tab, 16 * 5)

        @block.gpsimd
        def _(pool):
            nc.gpsimd.iota(iota_i[:, :], [[1, NP_]], base=0, channel_multiplier=0).then_inc(s_iota, 1)
            nc.gpsimd.iota(pid_i[:, :], [[0, 1]], base=0, channel_multiplier=1).then_inc(s_iota, 1)
            pool.wait_ge(s_ext, 1)
            nc.gpsimd.partition_all_reduce(extp[:, :, :].rearrange("p a s -> p (a s)"),
                                           ext[:, :, :].rearrange("p a s -> p (a s)"), P, RMAX).then_inc(s_extp, 1)
            for p in range(5):
                pool.sem_inc(g_used[p], 1) if False else None
                pool.wait_ge(s_tab, 16 * (p + 1))
                with pool.Fori(0, PAIRS) as i:
                    for b in range(2):
                        pool.wait_ge(idx_in[p][b], (i + 1) * 16)
                        pool.sem_inc(s_zero, 1)
                        for t in range(T):
                            nc.gpsimd.indirect_dma_start(
                                out=gb[:, b, t, 0:tabw[p]], out_offset=None, in_=tabs[p],
                                in_offset=bass.IndirectOffsetOnAxis(ap=idx[:, b, t:t + 1], axis=0)).then_inc(g_in[p][b], 16)

        @block.scalar
        def _(act):
            taken = [0]

            def root(out, in_):
                act.wait_ge(s_sqi, taken[0] + 1)
                nc.scalar.activation(out, in_, ACT.Sqrt).then_inc(s_sqo, 1)
                taken[0] += 1

            def node_root():
                root(r1_root[:, :], r1[:, :])

            def stat_root():
                root(sv_root[:, :], sv[:, 0:D])

            act.sem_inc(ea_cp, 2)
            root(rn_root, rn[:, :, :].rearrange("p s t -> p (s t)"))
            with act.Fori(0, PAIRS) as i:
                for b in range(2):
                    act.wait_ge(ea_in[b], (i + 1) * 16)
                    act.wait_ge(row_used[0], i * 2 + b + 1)
                    nc.scalar.activation(vals[:, b, :, 0:D], ea16[:, b, :, :], ACT.Copy).then_inc(ea_cp, 1)
            act.wait_ge(s_par, 16 * 21)
            node_root()
            node_root()
            for l in range(2):
                with act.Fori(0, PAIRS) as i:
                    for b in range(2):
                        for c in range(2):
                            act.wait_ge(h_mm[l], (i * 2 + b) * 2 + c + 1 + 3)
                            act.wait_ge(w_mm[l], (i * 2 + b) * 4 + c * 2 + 1)
                            nc.scalar.activation(ht[0:EK, b, c * 512:(c + 1) * 512], ps[0:EK, c, :], ACT.Relu,
                                                 bias=b1[l][:, 0:1]).then_inc(h_act[l], 1)
                stat_root()
                if l == 0:
                    stat_root()
                else:
                    node_root()
            stat_root()
            node_root()
            for k in range(2):
                act.wait_ge(s_thi, k + 1)
                nc.scalar.activation(hh[:, :, :], t1[:, :, 0:D], ACT.Tanh).then_inc(s_th, 1)
            node_root()

        @block.tensor
        def _(pe):
            def zero_bank(bk):
                return nc.tensor.matmul(ps[:, bk, :], zeros[:, 0:P], zeros[:, :], start=True, stop=False, skip_group_check=True)

            def window_matmuls(w, s, rhs_of, out_of):
                lo = pe.value_load(win[0:1, bass.ds(s, 1), 0], min_val=0, max_val=NB - 1)
                hi = pe.value_load(win[0:1, bass.ds(s, 1), 1], min_val=1, max_val=NB)
                off = pe.value_load(win[0:1, bass.ds(s, 1), 2], min_val=0, max_val=4096)
                with pe.Fori(lo, hi) as c:
                    for h in range(2):
                        pe.wait_ge(oh_ready[w][h], off + c + 1)
                        for u in range(T // 2):
                            mm = nc.tensor.matmul(out_of(c), onehot[:, h, u, :], rhs_of(h * (T // 2) + u),
                                                  start=False, stop=False, skip_group_check=True)
                        mm.then_inc(oh_used[w][h], 1)

            def partition_sum(k):
                pe.wait_ge(s_str, k + 1)
                nc.tensor.matmul(ps[:, 5, 0:32], ones[:, :], stat[:, :], start=True, stop=True,
                                 skip_group_check=True).then_inc(s_sts, 1)

            def node_product(k, rows, wts):
                K = wts.shape[0]
                pe.wait_ge(s_nmi, k + 1)
                for q in range(NB):
                    tr = nc.tensor.transpose(ps[0:K, TBANK[q // 4], (q % 4) * P:(q % 4 + 1) * P], rows(q), ident[:, :])
                tr.then_inc(s_nmt, 1)
                pe.wait_ge(s_nmc, (k + 1) * 7)
                for q in range(NB):
                    mm = nc.tensor.matmul(ps[:, 5, 64 + q * D:64 + (q + 1) * D], xt[0:K, q, :], wts,
                                          start=True, stop=True, skip_group_check=True)
                mm.then_inc(s_nmo, 1)

            pe.wait_ge(s_setup, 1)
            for w in range(4):
                for h in range(2):
                    pe.sem_inc(oh_used[w][h], BIAS + 1)
            for w in range(4):
                pe.sem_inc(row_used[w], 2)
            pe.wait_ge(s_par, 16 * 21)

            zero_bank(0)
            zero_bank(1)
            with pe.Fori(0, PAIRS) as i:
                for b in range(2):
                    s = i * 2 + b
                    pe.wait_ge(ea_cp, s + 3)
                    window_matmuls(0, s, lambda t: vals[:, b, t, :], lambda c: psf[:, bass.ds(c * 20, D + 1)])
                    pe.wait_ge(sc_oh, s + 1)
                    for t in range(T):
                        mm = nc.tensor.matmul(ps[:, 1, 0:NB], oh_lo[:, b, t, :], oh_hi[:, b, t, :],
                                              start=False, stop=False, skip_group_check=True)
                    mm.then_inc(row_used[0], 1)
            nc.tensor.matmul(ps[:, 2, 0:32], zeros[:, 0:P], zeros[:, 0:32], start=True, stop=True).then_inc(s_accd, 1)

            for l in range(2):
                W = MF if l == 0 else D
                HA = 13 if l == 0 else NB
                pe.wait_ge(s_node, l + 1)
                pe.sem_inc(h_mm[l], 3)
                pe.sem_inc(w_mm[l], 8)
                zero_bank(6)
                zero_bank(7)

                def scatter_tile(b, t):
                    obuf = big[:, b, t, :, :].rearrange("p h f -> p (h f)")
                    mm = nc.tensor.matmul(ps[:, 6, 0:HA * W], oh_lo[:, b, t, :], obuf[:, 0:HA * W],
                                          start=False, stop=False, skip_group_check=True)
                    if HA < NB:
                        mm = nc.tensor.matmul(ps[:, 7, 0:(NB - HA) * W], oh_lo[:, b, t, :], obuf[:, HA * W:NB * W],
                                              start=False, stop=False, skip_group_check=True)
                    mm.then_inc(sc_mm[l], 1)

                with pe.Fori(0, PAIRS) as i:
                    for b in range(2):
                        s = i * 2 + b
                        pe.wait_ge(eat_in[l][b], (i + 1) * 16)
                        for c in range(2):
                            pe.wait_ge(h_act[l], s * 2 + c + 1)
                            nc.tensor.matmul(ps[:, c, :], w1[l][:, :], eat[:, b, c * 512:(c + 1) * 512],
                                             start=True, stop=True).then_inc(h_mm[l], 1)
                        for g in range(4):
                            pe.wait_ge(h_act[l], s * 2 + g // 2 + 3)
                            pe.wait_ge(p_done[l], s * 4 + g + 1)
                            for u in range(2):
                                t = 2 * g + u
                                mm = nc.tensor.matmul(ps[:, 2 + t % 4, 0:MJ * D], ht[:, b, t * P:(t + 1) * P],
                                                      w2[l][:, :], start=True, stop=True)
                            mm.then_inc(w_mm[l], 1)
                            pe.wait_ge(o_done[l], s * 4 + g + 1)
                            scatter_tile(1 - b, 2 * g)
                            scatter_tile(1 - b, 2 * g + 1)
                pe.wait_ge(o_done[l], NSUP * 4 + 4)
                for t in range(T):
                    scatter_tile(1, t)
                nc.tensor.matmul(ps[:, 2, 0:32], zeros[:, 0:P], zeros[:, 0:32], start=True, stop=True).then_inc(s_accd, 1)
                if l == 0:
                    for k in range(3):
                        partition_sum(k)
                else:
                    for k in range(3, 5):
                        partition_sum(k)

            for p in range(2, 5):
                w = p - 1
                pe.wait_ge(s_node, p + 1)
                for bk in range(4):
                    zero_bank(bk)
                with pe.Fori(0, PAIRS) as i:
                    for b in range(2):
                        s = i * 2 + b
                        if p == 2:
                            pe.wait_ge(v_done, s + 1)
                            window_matmuls(w, s, lambda t: v48[:, b, t, :], lambda c: psf[:, bass.ds(c * 64, 3 * D)])
                        else:
                            pe.wait_ge(g_in[p][b], (i + 1) * 16 * T)
                            window_matmuls(w, s, lambda t: gb[:, b, t, 0:D], lambda c: psf[:, bass.ds(c * 64, D)])
                        mm = nc.tensor.matmul(ps[:, 6, 0:32], zeros[:, 0:P], zeros[:, 0:32], start=True, stop=True)
                        mm.then_inc(row_used[w] if p == 2 else g_used[p], 1)
                nc.tensor.matmul(ps[:, 6, 0:32], zeros[:, 0:P], zeros[:, 0:32], start=True, stop=True).then_inc(s_accd, 1)
                if p == 2:
                    node_product(0, lambda q: acc[:, q, :], wst[:, :])
                    for k in range(5, 7):
                        partition_sum(k)
                    node_product(1, lambda q: x[:, q, :], gw1[:, :])
                if p == 3:
                    node_product(2, lambda q: hh[:, q, :], gw2[:, :])

        @block.vector
        def _(dve):
            V = nc.vector
            chain = [0]

            def link(ins):
                chain[0] += 1
                ins.then_inc(s_dve, 1)
                dve.wait_ge(s_dve, chain[0])

            def bc(ap, n):
                return repeat(ap, len(ap.shape), n)

            roots = [2]

            def square_root(v, root, tmp, k):
                dve.wait_ge(s_sqo, k)
                link(V.tensor_scalar(tmp, root, 1e-30, None, ALU.max))
                link(V.reciprocal(tmp, tmp))
                link(V.tensor_tensor(tmp, tmp, v, ALU.mult))
                link(V.tensor_tensor(root, root, tmp, ALU.add))
                link(V.tensor_scalar(root, root, 0.5, None, ALU.mult))

            link(V.memset(zeros[:, :], 0.0))
            link(V.memset(ones[:, :], 1.0))
            link(V.memset(vals[:, :, :, :], 1.0))
            link(V.memset(ht[:, :, :], 1.0))
            link(V.memset(stat[:, :], 0.0))
            dve.wait_ge(s_iota, 2)
            link(V.tensor_copy(iota_f[:, :], iota_i[:, :]))
            link(V.tensor_copy(pid_f[:, :], pid_i[:, :]))
            link(V.tensor_scalar(ident[:, :], iota_f[:, 0:P], pid_f[:, 0:1], None, ALU.is_equal))
            link(V.tensor_scalar(node_id[:, :], iota_f[:, 0:NB], float(P), pid_f[:, 0:1], ALU.mult, ALU.add))
            link(V.tensor_scalar(mask[:, :], node_id[:, :], float(N), None, ALU.is_lt))
            dve.wait_ge(s_idx0, 64)
            link(V.tensor_copy(dst_f[:, :, :], dst_i[:, :, :]))
            link(V.tensor_scalar(neg_dst[:, :, :], dst_f[:, :, :], -1.0, None, ALU.mult))
            link(V.tensor_reduce(ext[:, 0, :], dst_f[:, :, :], AX.X, ALU.max))
            V.tensor_reduce(ext[:, 1, :], neg_dst[:, :, :], AX.X, ALU.max).then_inc(s_ext, 1)
            link(V.tensor_scalar(src_t[:, :, :], src_i[:, :, :], P - 1, None, ALU.bitwise_and))
            link(V.tensor_copy(src_lo[:, :, :], src_t[:, :, :]))
            link(V.tensor_scalar(src_t[:, :, :], src_i[:, :, :], 7, None, ALU.logical_shift_right))
            link(V.tensor_copy(src_hi[:, :, :], src_t[:, :, :]))
            dve.wait_ge(s_extp, 1)
            link(V.tensor_copy(ext_i[:, 0, :], extp[:, 0, :]))
            link(V.tensor_scalar(ext_i[:, 1, :], extp[:, 1, :], -1.0, None, ALU.mult))
            link(V.tensor_scalar(blk_i[:, :, :], ext_i[:, :, :], 7, None, ALU.logical_shift_right))
            link(V.tensor_copy(blk[:, :, :], blk_i[:, :, :]))
            link(V.tensor_tensor(cnt_w[:, :], blk[:, 0, :], blk[:, 1, :], ALU.subtract))
            link(V.tensor_scalar(cnt_w[:, :], cnt_w[:, :], 1.0, None, ALU.add))
            link(V.tensor_tensor_scan(cum_w[:, :], ones[:, 0:NSUP], cnt_w[:, :], 0.0, ALU.mult, ALU.add))
            link(V.memset(win_f[:, :, :], 0.0))
            link(V.tensor_copy(win_f[:, :, 0], blk[:, 1, :]))
            link(V.tensor_scalar(win_f[:, :, 1], blk[:, 0, :], 1.0, None, ALU.add))
            link(V.tensor_tensor(cum_w[:, :], cum_w[:, :], cnt_w[:, :], ALU.subtract))
            link(V.tensor_tensor(cum_w[:, :], cum_w[:, :], blk[:, 1, :], ALU.subtract))
            link(V.tensor_scalar(win_f[:, :, 2], cum_w[:, :], float(BIAS), None, ALU.add))
            link(V.tensor_copy(win[:, :, :], win_f[:, :, :]))
            for w in range(4):
                for h in range(2):
                    dve.sem_inc(oh_ready[w][h], BIAS)
            link(V.memset(sv[:, :], 1.0))
            V.memset(sm[:, :], 0.0).then_inc(s_setup, 1)

            rv = rhat[:, :, :, :].rearrange("p s t c -> p (s t) c")
            rnf = rn[:, :, :].rearrange("p s t -> p (s t)")
            rq = rsq.rearrange("p (n c) -> p n c", c=3)
            link(V.tensor_tensor(rq, rv, rv, ALU.mult))
            V.tensor_reduce(rnf, rq, AX.X, ALU.add).then_inc(s_sqi, 1)
            square_root(rnf, rn_root, rn_t, 1)
            link(V.tensor_scalar(rnf, rn_root, 1e-12, None, ALU.add))
            link(V.reciprocal(rnf, rnf))
            link(V.tensor_tensor(rv, rv, bc(rnf, 3), ALU.mult))

            def window_onehots(w, s):
                lo = dve.value_load(win[0:1, bass.ds(s, 1), 0], min_val=0, max_val=NB - 1)
                hi = dve.value_load(win[0:1, bass.ds(s, 1), 1], min_val=1, max_val=NB)
                off = dve.value_load(win[0:1, bass.ds(s, 1), 2], min_val=0, max_val=4096)
                with dve.Fori(lo, hi) as c:
                    for h in range(2):
                        dve.wait_ge(oh_used[w][h], off + c + 1)
                        d = dst_f[:, bass.ds(s, 1), h * 4:h * 4 + 4].rearrange("p o t -> p (o t)")
                        cols = repeat(iota_f[:, bass.ds(c * P, P)], 1, T // 2)
                        V.tensor_tensor(onehot[:, h, :, :], bc(d, P), cols, ALU.is_equal).then_inc(oh_ready[w][h], 1)

            def one_sup(ap3, s):
                return ap3[:, bass.ds(s, 1), :].rearrange("p o t -> p (o t)")

            def source_onehots(b, s, last_sem):
                lo = one_sup(src_lo, s)
                hi = one_sup(src_hi, s)
                V.tensor_tensor(oh_lo[:, b, :, :], bc(lo, P), repeat(iota_f[:, 0:P], 1, T), ALU.is_equal)
                V.tensor_tensor(oh_hi[:, b, :, :], bc(hi, NB), repeat(iota_f[:, 0:NB], 1, T),
                                ALU.is_equal).then_inc(last_sem, 1)

            with dve.Fori(0, PAIRS) as i:
                for b in range(2):
                    s = i * 2 + b
                    window_onehots(0, s)
                    dve.wait_ge(row_used[0], s + 1)
                    source_onehots(b, s, sc_oh)

            def layer_norm(xx):
                link(V.tensor_reduce(r1[:, :], xx, AX.X, ALU.add))
                link(V.tensor_scalar(r1[:, :], r1[:, :], 1.0 / D, None, ALU.mult))
                link(V.tensor_tensor(xx, xx, bc(r1[:, :], D), ALU.subtract))
                link(V.tensor_tensor(t2[:, :, 0:D], xx, xx, ALU.mult))
                link(V.tensor_reduce(r1[:, :], t2[:, :, 0:D], AX.X, ALU.add))
                roots[0] += 1
                V.tensor_scalar(r1[:, :], r1[:, :], 1.0 / D, EPS, ALU.mult, ALU.add).then_inc(s_sqi, 1)
                square_root(r1[:, :], r1_root[:, :], r1_t[:, :], roots[0])
                link(V.reciprocal(r1[:, :], r1_root[:, :]))
                link(V.tensor_tensor(xx, xx, bc(r1[:, :], D), ALU.mult))

            stats = [0]

            def node_sum(src, n):
                V.tensor_reduce(stat[:, 0:n], src.rearrange("p q f -> p f q"), AX.X, ALU.add).then_inc(s_str, 1)
                stats[0] += 1
                dve.wait_ge(s_sts, stats[0])

            def over_nodes(ap, f):
                return repeat(ap, 1, NB)

            def batch_norm(xx, g, b_):
                node_sum(xx, D)
                link(V.tensor_scalar(sm[:, 0:D], ps[:, 5, 0:D], 1.0 / N, None, ALU.mult))
                link(V.tensor_tensor(xx, xx, over_nodes(sm[:, 0:D], D), ALU.subtract))
                link(V.tensor_tensor(xx, xx, bc(mask[:, :], D), ALU.mult))
                link(V.tensor_tensor(t2[:, :, 0:D], xx, xx, ALU.mult))
                node_sum(t2[:, :, 0:D], D)
                roots[0] += 1
                V.tensor_scalar(sv[:, 0:D], ps[:, 5, 0:D], 1.0 / N, EPS, ALU.mult, ALU.add).then_inc(s_sqi, 1)
                square_root(sv[:, 0:D], sv_root[:, :], sv_t[:, :], roots[0])
                link(V.reciprocal(sv[:, 0:D], sv_root[:, :]))
                link(V.tensor_tensor(sv[:, 0:D], sv[:, 0:D], par[:, g, :], ALU.mult))
                link(V.tensor_tensor(xx, xx, over_nodes(sv[:, 0:D], D), ALU.mult))
                link(V.tensor_tensor(xx, xx, over_nodes(par[:, b_, :], D), ALU.add))

            dve.wait_ge(s_accd, 1)
            dve.wait_ge(s_x, 16)
            dve.wait_ge(s_par, 16 * 21)
            a0 = ps[:, 0, 0:NB * 20].rearrange("p (q f) -> p q f", f=20)
            V.tensor_scalar(r1[:, :], a0[:, :, D], 1.0, None, ALU.add).then_inc(s_sqi, 1)
            square_root(r1[:, :], r1_root[:, :], r1_t[:, :], 2)
            link(V.reciprocal(dinv[:, :], r1_root[:, :]))
            link(V.tensor_scalar(rcd[:, :], a0[:, :, D], 1.0, None, ALU.max))
            link(V.reciprocal(rcd[:, :], rcd[:, :]))
            link(V.tensor_scalar(rcs[:, :], ps[:, 1, 0:NB], 1.0, None, ALU.max))
            link(V.reciprocal(rcs[:, :], rcs[:, :]))
            link(V.tensor_tensor(rcs[:, :], rcs[:, :], mask[:, :], ALU.mult))
            link(V.tensor_tensor(t1[:, :, 0:D], a0[:, :, 0:D], bc(rcd[:, :], D), ALU.mult))
            link(V.tensor_tensor(x[:, :, :], x[:, :, :], t1[:, :, 0:D], ALU.add))
            layer_norm(x[:, :, :])
            V.tensor_copy(tab[:, :, 0:D], x[:, :, :]).then_inc(s_tabr, 1)
            link(V.memset(big[:, :, :, :, :].rearrange("p b t h f -> p (b t h f)"), 0.0))
            dve.sem_inc(s_node, 1)

            for l in range(2):
                p = l
                dve.sem_inc(h_act[l], 2)
                dve.sem_inc(p_done[l], 2)
                dve.sem_inc(r_done[l], 2)
                dve.sem_inc(o_done[l], 4)
                dve.sem_inc(sc_mm[l], 8)
                dve.sem_inc(g_used[l], 2)
                W = MF if l == 0 else D
                I_, J_ = (D, MJ) if l == 0 else (MJ, D)
                with dve.Fori(0, PAIRS) as i:
                    for b in range(2):
                        s = i * 2 + b
                        rh = rhat[:, bass.ds(s, 1), :, :].rearrange("p o t c -> p (o t) c")
                        dve.wait_ge(g_in[p][b], (i + 1) * 16 * T)
                        if l == 1:
                            V.tensor_tensor(vprod[:, :, :, :], gb[:, b, :, 0:12].rearrange("p t (j c) -> p t j c", c=3),
                                            repeat(rh, 2, NV), ALU.mult).then_inc(q_done[l], 1)
                            dve.wait_ge(q_done[l], s * 2 + 1)
                            V.tensor_reduce(gb[:, b, :, 28:32], vprod[:, :, :, :], AX.X, ALU.add).then_inc(q_done[l], 1)
                            dve.wait_ge(q_done[l], s * 2 + 2)
                        for g in range(4):
                            dve.wait_ge(w_mm[l], s * 4 + g + 9)
                            dve.wait_ge(r_done[l], s * 4 + g + 1)
                            xin = gb[:, b, 2 * g:2 * g + 2, 0:D] if l == 0 else gb[:, b, 2 * g:2 * g + 2, 12:32]
                            wv = ps[:, 2 + (2 * g) % 4:4 + (2 * g) % 4, 0:MJ * D].rearrange("p t (i j) -> p t i j", j=J_)
                            pv = prod[:, g % 2, :, :].rearrange("p t (i j) -> p t i j", j=J_)
                            pr = V.tensor_tensor(pv, wv, bc(xin, J_), ALU.mult).then_inc(p_done[l], 1)
                            if g == 0:
                                dve.wait_ge(o_done[l], s * 4 + 1)
                            dve.wait_ge(p_done[l], s * 4 + g + 3)
                            V.tensor_reduce(msg[:, b, 2 * g:2 * g + 2, 0:J_], pv.rearrange("p t i j -> p t j i"),
                                            AX.X, ALU.add).then_inc(r_done[l], 1)
                        if l == 0:
                            dve.wait_ge(r_done[l], s * 4 + 6)
                            V.tensor_tensor(msg[:, b, :, MJ:MJ + 12].rearrange("p t (j c) -> p t j c", c=3),
                                            bc(msg[:, b, :, 0:NV], 3), repeat(rh, 2, NV),
                                            ALU.mult).then_inc(q_done[l], 1)
                        dve.wait_ge(sc_mm[l], s * 8 + 1)
                        source_onehots(b, s, l_done[l])
                        dve.wait_ge(l_done[l], s + 1)
                        if l == 0:
                            dve.wait_ge(q_done[l], s + 1)
                        else:
                            dve.wait_ge(r_done[l], s * 4 + 6)
                        for g in range(4):
                            ob = big[:, b, 2 * g:2 * g + 2, :, :].rearrange("p t h f -> p t (h f)")[:, :, 0:NB * W]
                            m0 = NV if l == 0 else 0
                            last = V.tensor_tensor(ob.rearrange("p t (h f) -> p t h f", f=W),
                                                   repeat(msg[:, b, 2 * g:2 * g + 2, m0:m0 + W], 2, NB),
                                                   bc(oh_hi[:, b, 2 * g:2 * g + 2, :], W), ALU.mult)
                            last.then_inc(o_done[l], 1)
                        dve.sem_inc(g_used[l], 1)
                dve.wait_ge(s_accd, l + 2)
                if l == 0:
                    link(V.tensor_scalar(rn[:, 0, 0:1], rn[:, 0, 0:1], 1.0, None, ALU.mult))
                    for bank, q0, q1 in ((6, 0, 13), (7, 13, NB)):
                        av = ps[:, bank, 0:(q1 - q0) * MF].rearrange("p (q f) -> p q f", f=MF)
                        link(V.tensor_tensor(t1[:, q0:q1, 0:MF], av, bc(rcs[:, q0:q1], MF), ALU.mult))
                    link(V.tensor_scalar(tab[:, :, 12:MF], t1[:, :, 0:D], 0.25, None, ALU.mult))
                    link(V.tensor_scalar(tab[:, :, 0:12], t1[:, :, D:MF], 0.25 * 3.0 ** 0.5, None, ALU.mult))
                    batch_norm(tab[:, :, 12:MF], GS0, BS0)
                    link(V.tensor_tensor(t2[:, :, 0:12], tab[:, :, 0:12], tab[:, :, 0:12], ALU.mult))
                    node_sum(t2[:, :, 0:12], 12)
                    link(V.tensor_copy(sm[:, 0:12], ps[:, 5, 0:12]))
                    link(V.tensor_reduce(sv[:, 0:NV], sm[:, 0:12].rearrange("p (j c) -> p j c", c=3), AX.X, ALU.add))
                    roots[0] += 1
                    V.tensor_scalar(sv[:, 0:D], sv[:, 0:D], 1.0 / (3 * N), EPS, ALU.mult, ALU.add).then_inc(s_sqi, 1)
                    square_root(sv[:, 0:D], sv_root[:, :], sv_t[:, :], roots[0])
                    link(V.reciprocal(sv[:, 0:D], sv_root[:, :]))
                    link(V.tensor_tensor(sv[:, 0:NV], sv[:, 0:NV], par[:, GV0, 0:NV], ALU.mult))
                    link(V.tensor_copy(sm[:, 0:12].rearrange("p (j c) -> p j c", c=3), bc(sv[:, 0:NV], 3)))
                    V.tensor_tensor(tab[:, :, 0:12], tab[:, :, 0:12], over_nodes(sm[:, 0:12], 12), ALU.mult).then_inc(s_tabr, 1)
                    link(V.memset(big[:, :, :, :, :].rearrange("p b t h f -> p (b t h f)"), 0.0))
                    dve.sem_inc(s_node, 1)
                else:
                    av = ps[:, 6, 0:NB * D].rearrange("p (q f) -> p q f", f=D)
                    link(V.tensor_tensor(t1[:, :, 0:D], av, bc(rcs[:, :], D), ALU.mult))
                    link(V.tensor_scalar(t1[:, :, 0:D], t1[:, :, 0:D], float(MJ) ** -0.5, None, ALU.mult))
                    batch_norm(t1[:, :, 0:D], GS1, BS1)
                    link(V.tensor_tensor(x[:, :, :], x[:, :, :], t1[:, :, 0:D], ALU.add))
                    layer_norm(x[:, :, :])
                    dve.wait_ge(s_tab, 32)
                    V.tensor_copy(tab[:, :, 0:D], x[:, :, :]).then_inc(s_tabr, 1)
                    dve.sem_inc(s_node, 1)

            products = [0]

            def node_product(K):
                k = products[0]
                products[0] += 1
                dve.wait_ge(s_nmt, k + 1)
                for j in range(7):
                    n = min(4, NB - 4 * j)
                    V.tensor_copy(xt[0:K, 4 * j:4 * j + n, :],
                                  ps[0:K, TBANK[j], 0:n * P].rearrange("k (n c) -> k n c", c=P)).then_inc(s_nmc, 1)
                dve.wait_ge(s_nmo, k + 1)
                return ps[:, 5, 64:64 + NB * D].rearrange("p (q f) -> p q f", f=D)

            for p in range(2, 5):
                w = p - 1
                dve.sem_inc(g_used[p], 2)
                with dve.Fori(0, PAIRS) as i:
                    for b in range(2):
                        s = i * 2 + b
                        if p == 2:
                            dve.wait_ge(g_in[p][b], (i + 1) * 16 * T)
                            dve.wait_ge(row_used[w], s + 1)
                            for k in range(2):
                                ek = ea2[:, bass.ds(s, 1), :, k].rearrange("p o t -> p (o t)")
                                V.tensor_tensor(v48[:, b, :, k * D:(k + 1) * D], gb[:, b, :, 0:D], bc(ek, D), ALU.mult)
                            V.tensor_copy(v48[:, b, :, 2 * D:3 * D], gb[:, b, :, 0:D]).then_inc(v_done, 1)
                            dve.wait_ge(v_done, s + 1)
                            dve.sem_inc(g_used[p], 1)
                        window_onehots(w, s)
                dve.wait_ge(s_accd, p + 2)
                av = psf[:, 0:NB * 64].rearrange("p (q f) -> p q f", f=64)
                if p == 2:
                    link(V.tensor_tensor(acc[:, :, 0:3 * D], av[:, :, 0:3 * D], bc(rcd[:, :], 3 * D), ALU.mult))
                    V.tensor_copy(acc[:, :, 3 * D:4 * D], x[:, :, :]).then_inc(s_nmi, 1)
                    res = node_product(4 * D)
                    link(V.tensor_tensor(t1[:, :, 0:D], res, over_nodes(par[:, B2, :], D), ALU.add))
                    link(V.tensor_tensor(t1[:, :, 0:D], t1[:, :, 0:D], bc(mask[:, :], D), ALU.mult))
                    batch_norm(t1[:, :, 0:D], GA, BE)
                    link(V.scalar_tensor_tensor(out=t2[:, :, 0:D], in0=t1[:, :, 0:D], scalar=0.01, in1=t1[:, :, 0:D],
                                                op0=ALU.mult, op1=ALU.max))
                    link(V.tensor_tensor(t2[:, :, 0:D], t2[:, :, 0:D], x[:, :, :], ALU.add))
                    link(V.tensor_tensor(x[:, :, :], t2[:, :, 0:D], x[:, :, :], ALU.add))
                    layer_norm(x[:, :, :])
                    dve.sem_inc(s_nmi, 1)
                    res = node_product(D)
                    dve.wait_ge(s_tab, 48)
                    V.tensor_tensor(tab[:, :, 0:D], res, bc(dinv[:, :], D), ALU.mult).then_inc(s_tabr, 1)
                    dve.wait_ge(s_tabr, p + 2)
                    dve.sem_inc(s_node, 1)
                else:
                    link(V.tensor_tensor(t2[:, :, 0:D], av[:, :, 0:D], tab[:, :, 0:D], ALU.add))
                    link(V.tensor_tensor(t2[:, :, 0:D], t2[:, :, 0:D], bc(dinv[:, :], D), ALU.mult))
                    V.tensor_tensor(t1[:, :, 0:D], t2[:, :, 0:D],
                                    over_nodes(par[:, C1, :] if p == 3 else c2[:, :], D), ALU.add).then_inc(s_thi, 1)
                    dve.wait_ge(s_th, p - 2)
                    if p == 3:
                        dve.sem_inc(s_nmi, 1)
                        res = node_product(D)
                        dve.wait_ge(s_tab, 64)
                        V.tensor_tensor(tab[:, :, 0:D], res, bc(dinv[:, :], D), ALU.mult).then_inc(s_tabr, 1)
                        dve.wait_ge(s_tabr, p + 2)
                        dve.sem_inc(s_node, 1)
                    else:
                        link(V.tensor_tensor(x[:, :, :], x[:, :, :], hh[:, :, :], ALU.add))
                        layer_norm(x[:, :, :])
                        dve.sem_inc(s_fin, 1)


def kernel(**inputs):
    import numpy as np
    import concourse.bacc as bacc
    from concourse import mybir as mb
    from concourse.bass_utils import run_bass_kernel_spmd as run

    g = {k: np.asarray(v) for k, v in inputs.items()}

    def pad_rows(v, n, fill=0):
        out = np.full((n,) + v.shape[1:], fill, v.dtype)
        out[:v.shape[0]] = v
        return out

    arrays = {
        "x": pad_rows(g["x"], NP_),
        "src": pad_rows(g["src"], EP, DUMP),
        "dst": pad_rows(g["dst"], EP, DUMP),
        "edge_attr_2": pad_rows(g["edge_attr_2"], EP),
        "edge_attr_3": pad_rows(g["edge_attr_3"], EP),
        "edge_attr_16": pad_rows(g["edge_attr_16"], EP),
        "eat": pad_rows(g["edge_attr_48"], EP).reshape(NSUP, P, T, EK).transpose(0, 3, 2, 1).reshape(NSUP, EK, SUP),
    }
    for l in range(2):
        w2 = np.concatenate([g[f"L1_gnn_fc{l}_w2"], g[f"L1_gnn_fc{l}_b2"][None]], axis=0)
        if l == 0:
            wa = w2[:, :D * D].reshape(EK + 1, D, D)
            wb = w2[:, D * D:].reshape(EK + 1, D, NV)
            w2 = np.concatenate([wb, wa], axis=2).reshape(EK + 1, D * MJ)
        arrays[f"w2_{l}"] = w2
        w1 = np.zeros((EK, P), np.float32)
        w1[:, :EK] = g[f"L1_gnn_fc{l}_w1"]
        arrays[f"w1_{l}"] = w1
        arrays[f"b1_{l}"] = g[f"L1_gnn_fc{l}_b1"]
    arrays["w_enet"] = g["L2_gnn_W_enet"].reshape(2 * D, D)
    arrays["b_enet"] = g["L2_gnn_b_enet"].reshape(D, D)
    arrays["w_root"] = g["L2_gnn_W_root"]
    arrays["gw1"] = g["L3_gnn_W1"]
    arrays["gw2"] = g["L3_gnn_W2"]
    for short, full in (("gs0", "L1_gnn_bn0_gs"), ("bs0", "L1_gnn_bn0_bs"), ("gv0", "L1_gnn_bn0_gv"),
                        ("gs1", "L1_gnn_bn1_gs"), ("bs1", "L1_gnn_bn1_bs"), ("bias", "L2_gnn_bias"),
                        ("gamma", "L2_gnn_gamma"), ("beta", "L2_gnn_beta"), ("gb1", "L3_gnn_b1"), ("gb2", "L3_gnn_b2")):
        arrays[short] = g[full]
    nc = bacc.Bacc("TRN2", target_bir_lowering=False, num_devices=1)
    feeds, aps = {}, {}
    for name, v in arrays.items():
        v = np.ascontiguousarray(v)
        feeds[f"in_{name}"] = v
        aps[name] = nc.dram_tensor(f"in_{name}", v.shape, mb.dt.from_np(v.dtype), kind="ExternalInput").ap()
    aps["out"] = nc.dram_tensor("out_x", (N, D), mb.dt.float32, kind="ExternalOutput").ap()
    build(nc, aps)
    r = run(nc, [feeds], core_ids=[0])
    return r.results[0]["out_x"]
```

```python
from contextlib import ExitStack

import concourse.bass as bass
from concourse import mybir

ALU = mybir.AluOpType
ACT = mybir.ActivationFunctionType
AX = mybir.AxisListType
F32 = mybir.dt.float32
BF16 = mybir.dt.bfloat16
I32 = mybir.dt.int32
F32R = mybir.dt.float32r
RMAX = bass.bass_isa.ReduceOp.max

P = 128
N = 3125
E = 100000
D = 16
NB = -(-N // P)
NP_ = NB * P
T = 8
SUP = T * P
NSUP = 98
EP = NSUP * SUP
PAIRS = NSUP // 2
EK = 48
NV = 4
MJ = D + NV
MF = D + 3 * NV
EPS = 1e-5
DUMP = NP_ - 1
NC = 5
NH = NB // NC
CW = NC * P
AT = 6
MP = [2 * (MF + 1), 2 * D]
BIAS = NB - 1
assert NSUP % 2 == 0 and EP >= E and NP_ > N


def repeat(ap, axis, n):
    wide = ap.unsqueeze(axis)
    shape = list(wide.shape)
    shape[axis] = n
    return wide.broadcast_to(shape)


def build(nc, a):
    with ExitStack() as ctx:
        def sb(name, shape, dt=F32):
            return ctx.enter_context(nc.sbuf_tensor(name, shape, dt))

        def sem(name):
            return ctx.enter_context(nc.semaphore(name))

        dst_i = sb("dst_i", [P, NSUP, T], I32)
        dst_f = sb("dst_f", [P, NSUP, T])
        src_i = sb("src_i", [P, NSUP, T], I32)
        src_f = sb("src_f", [P, NSUP, T])
        src_h = sb("src_h", [P, NSUP, T])
        src_v = sb("src_v", [P, NSUP, T])
        src_n = sb("src_n", [P, NSUP, T])
        rhat = sb("rhat", [P, NSUP, T, 3])
        rn = sb("rn", [P, NSUP, T])
        ea2 = sb("ea2", [P, NSUP, T, 2])
        big = sb("big", [P, 2, T, NH * MP[0]], F32R)
        oh5 = sb("oh5", [P, 2, T, CW], F32R)
        xt = sb("xt", [P, NB, P])
        xtf = xt[:, :, :].rearrange("p q c -> p (q c)")
        iota_i = xtf.bitcast(I32)
        rsq = xtf[:, 0:NSUP * T * 3]
        iota_f = sb("iota_f", [P, NP_])
        pid_i = sb("pid_i", [P, 1], I32)
        pid_f = sb("pid_f", [P, 1])
        ident = sb("ident", [P, P])
        ones = sb("ones", [P, P])
        zeros = sb("zeros", [P, 512], BF16)
        mask = sb("mask", [P, NB])
        node_id = sb("node_id", [P, NB])
        ext = sb("ext", [P, 2, NSUP])
        extp = sb("extp", [P, 2, NSUP])
        ext_i = sb("ext_i", [P, 2, NSUP], I32)
        blk_i = sb("blk_i", [P, 2, NSUP], I32)
        blk = sb("blk", [P, 2, NSUP])
        cnt_w = sb("cnt_w", [P, NSUP])
        cum_w = sb("cum_w", [P, NSUP])
        win_f = sb("win_f", [P, NSUP])
        win = sb("win", [P, NSUP], I32)
        neg_dst = rn

        ea16 = sb("ea16", [P, 2, T, D])
        vals = sb("vals", [P, 2, T, 2 * (D + 1)], F32R)
        oh_r = sb("oh_r", [P, 2, T // 2, P], F32R)
        oh_b = sb("oh_b", [P, 2, T // 2, P], BF16)
        oh_h = sb("oh_h", [P, 2, T, NH])
        eat = sb("eat", [P, 2, SUP])
        ht = sb("ht", [P, 2, SUP])
        idx = sb("idx", [P, 2, T], I32)
        gb = sb("gb", [P, 2, T, 32])
        vprod = sb("vprod", [P, T, NV, 3])
        prod = sb("prod", [P, 4, MJ * D])
        msg = sb("msg", [P, 2, T, 32])
        parts = [sb(f"parts{l}", [P, 2, T, MP[l]], F32R) for l in range(2)]
        v48 = sb("v48", [P, 2, T, 3 * D])
        v96 = sb("v96", [P, 2, T, 2, 3 * D], F32R)
        tabb = sb("tabb", [P, NB, 3, D], BF16)
        w1 = [sb(f"w1_{l}", [P, P]) for l in range(2)]
        b1 = [sb(f"b1_{l}", [EK, 1]) for l in range(2)]
        w2 = [sb(f"w2_{l}", [P, MJ * D]) for l in range(2)]
        par = sb("par", [P, 9, D])
        GS0, BS0, GV0, GS1, BS1, B2, GA, BE, C1 = range(9)
        c2 = sb("c2", [P, D])
        wst = sb("wst", [4 * D, D])
        gw1 = sb("gw1", [D, D])
        gw2 = sb("gw2", [D, D])

        x = sb("x", [P, NB, D])
        acc = sb("acc", [P, NB, 64])
        t1 = sb("t1", [P, NB, 32])
        t2 = sb("t2", [P, NB, 32])
        r1 = sb("r1", [P, NB])
        rcd = sb("rcd", [P, NB])
        rcs = sb("rcs", [P, NB])
        dinv = sb("dinv", [P, NB])
        tab = sb("tab", [P, NB, 32])
        hh = sb("hh", [P, NB, D])
        stat = sb("stat", [P, 32])
        sm = sb("sm", [P, 32])
        sv = sb("sv", [P, 32])
        r1_root = sb("r1_root", [P, NB])
        r1_t = sb("r1_t", [P, NB])
        sv_root = sb("sv_root", [P, D])
        sv_t = sb("sv_t", [P, D])
        rn_root = xtf[:, 0:NSUP * T]
        rn_t = xtf[:, NSUP * T:2 * NSUP * T]

        ps = ctx.enter_context(nc.psum_tensor("ps", [P, 8, 512], F32))
        psf = ps[:, :, :].rearrange("p b n -> p (b n)")
        TBANK = [0, 1, 2, 3, 4, 6, 7]

        s_par = sem("s_par")
        s_pad = sem("s_pad")
        s_idx0 = sem("s_idx0")
        s_x = sem("s_x")
        s_iota = sem("s_iota")
        s_dve = sem("s_dve")
        s_ext = sem("s_ext")
        s_extp = sem("s_extp")
        s_setup = sem("s_setup")
        s_node = sem("s_node")
        s_tab = sem("s_tab")
        s_tabr = sem("s_tabr")
        s_str = sem("s_str")
        s_sts = sem("s_sts")
        s_nmi = sem("s_nmi")
        s_nmt = sem("s_nmt")
        s_nmc = sem("s_nmc")
        s_nmo = sem("s_nmo")
        s_accd = sem("s_accd")
        s_zero = sem("s_zero")
        s_th = sem("s_th")
        s_sqi = sem("s_sqi")
        s_sqo = sem("s_sqo")
        s_thi = sem("s_thi")
        s_fin = sem("s_fin")
        s_out = sem("s_out")

        oh_ready = [[sem(f"oh_ready{p}_{h}") for h in range(2)] for p in range(4)]
        oh_used = [[sem(f"oh_used{p}_{h}") for h in range(2)] for p in range(4)]
        row_used = [sem(f"row_used{p}") for p in range(4)]
        ea_in = [sem(f"ea_in{b}") for b in range(2)]
        ea_cp = sem("ea_cp")
        ea_lo = sem("ea_lo")
        idx_in = [[sem(f"idx_in{p}_{b}") for b in range(2)] for p in range(5)]
        g_in = [[sem(f"g_in{p}_{b}") for b in range(2)] for p in range(5)]
        g_used = {p: sem(f"g_used{p}") for p in (3, 4)}
        eat_in = [[sem(f"eat_in{l}_{b}") for b in range(2)] for l in range(2)]
        h_mm = [sem(f"h_mm{l}") for l in range(2)]
        h_act = [sem(f"h_act{l}") for l in range(2)]
        w_mm = [sem(f"w_mm{l}") for l in range(2)]
        p_done = [sem(f"p_done{l}") for l in range(2)]
        r_done = [sem(f"r_done{l}") for l in range(2)]
        q_done = [sem(f"q_done{l}") for l in range(2)]
        m_hi = [sem(f"m_hi{l}") for l in range(2)]
        m_lo = [sem(f"m_lo{l}") for l in range(2)]
        l_done = [sem(f"l_done{l}") for l in range(2)]
        a_abs = [sem(f"a_abs{l}") for l in range(2)]
        a_done = [sem(f"a_done{l}") for l in range(2)]
        o_done = [sem(f"o_done{l}") for l in range(2)]
        sc_mm = [sem(f"sc_mm{l}") for l in range(2)]
        vp_done = sem("vp_done")
        vh_done = sem("vh_done")
        vl_done = sem("vl_done")

        tabs = [nc.dram_tensor(f"table{p}", (NP_, w), F32, kind="Internal").ap()
                for p, w in enumerate([D, MF, D, 3 * D // 2, 3 * D // 2])]
        tabw = [D, MF, D, 3 * D // 2, 3 * D // 2]
        tabbf = tabb[:, :, :, :].rearrange("p q k f -> p q (k f)").bitcast(F32)

        block = ctx.enter_context(nc.Block())

        e3 = a["edge_attr_3"].rearrange("(s p t) c -> p s (t c)", p=P, t=T)
        e2 = a["edge_attr_2"].rearrange("(s p t) c -> p s (t c)", p=P, t=T)
        e16 = a["edge_attr_16"].rearrange("(s p t) c -> s p (t c)", p=P, t=T)
        srcv = a["src"].rearrange("(s p t) -> p s t", p=P, t=T)
        dstv = a["dst"].rearrange("(s p t) -> p s t", p=P, t=T)
        gidx = [a["dst"], a["dst"], a["src"], a["src"], a["src"]]
        gidxv = [g.rearrange("(s p t) -> s p t", p=P, t=T) for g in gidx]
        WIN = {0: 0, 2: 1, 3: 2, 4: 3}

        def load_window(eng, s):
            word = eng.value_load(win[0:1, bass.ds(s, 1)], min_val=0, max_val=(1 << 23) - 1)
            lo = eng.snap(word & 31, min_val=0, max_val=NB - 1)
            hi = eng.snap((word >> 5) & 31, min_val=1, max_val=NB)
            off = eng.snap(word >> 10, min_val=0, max_val=4096)
            return lo, hi, off

        @block.sync
        def _(sp):
            sp.dma_start(dst_i[:, :, :], dstv).then_inc(s_idx0, 16)
            sp.dma_start(src_i[:, :, :], srcv).then_inc(s_idx0, 16)
            sp.dma_start(rhat[:, :, :, :].rearrange("p s t c -> p s (t c)"), e3).then_inc(s_idx0, 16)
            sp.dma_start(ea2[:, :, :, :].rearrange("p s t c -> p s (t c)"), e2).then_inc(s_idx0, 16)
            sp.dma_start(x[:, :, :], a["x"].rearrange("(q p) f -> p q f", p=P)).then_inc(s_x, 16)
            sp.wait_ge(s_pad, 1)
            for l in range(2):
                sp.dma_start(w1[l][0:EK, :], a[f"w1_{l}"]).then_inc(s_par, 16)
                sp.dma_start(b1[l][:, :], a[f"b1_{l}"].rearrange("(k o) -> k o", o=1)).then_inc(s_par, 16)
                sp.dma_start(w2[l][0:EK + 1, :], a[f"w2_{l}"]).then_inc(s_par, 16)
            sp.dma_start(wst[0:2 * D, :], a["w_enet"]).then_inc(s_par, 16)
            sp.dma_start(wst[2 * D:3 * D, :], a["b_enet"]).then_inc(s_par, 16)
            sp.dma_start(wst[3 * D:4 * D, :], a["w_root"]).then_inc(s_par, 16)
            sp.dma_start(gw1[:, :], a["gw1"]).then_inc(s_par, 16)
            sp.dma_start(gw2[:, :], a["gw2"]).then_inc(s_par, 16)
            for i, n in enumerate(["gs0", "bs0", "gv0", "gs1", "bs1", "bias", "gamma", "beta", "gb1"]):
                k = a[n].shape[0]
                sp.dma_start(par[:, i, 0:k], a[n].rearrange("(o k) -> o k", o=1).broadcast_to([P, k])).then_inc(s_par, 16)
            sp.dma_start(c2[:, :], a["gb2"].rearrange("(o k) -> o k", o=1).broadcast_to([P, D])).then_inc(s_par, 16)

            with sp.Fori(0, PAIRS) as i:
                for b in range(2):
                    sp.wait_ge(ea_lo, i * 2 + b + 1)
                    sp.dma_start(ea16[:, b, :, :].rearrange("p t f -> p (t f)"),
                                 e16[bass.ds(i * 2 + b, 1), :, :].rearrange("o p f -> p (o f)")).then_inc(ea_in[b], 16)

            def store_table(p):
                sp.wait_ge(s_tabr, p + 1)
                rows = tab[:, :, 0:tabw[p]] if p < 3 else tabbf
                sp.dma_start(tabs[p].rearrange("(q p) f -> p q f", p=P), rows).then_inc(s_tab, 16)

            def load_idx(p, b, s):
                sp.dma_start(idx[:, b, :], gidxv[p][bass.ds(s, 1), :, :].rearrange("o p t -> p (o t)")).then_inc(idx_in[p][b], 16)

            def load_eat(l, b, s):
                sp.wait_ge(h_mm[l], s * 2 + 1)
                sp.dma_start(eat[0:EK, b, :], a["eat"][bass.ds(s, 1), :, :].rearrange("o k n -> k (o n)")).then_inc(eat_in[l][b], 16)

            for p in range(5):
                store_table(p)
                for b in range(2):
                    if p < 2:
                        load_eat(p, b, b)
                    load_idx(p, b, b)
                with sp.Fori(1, PAIRS) as i:
                    for b in range(2):
                        if p < 2:
                            load_eat(p, b, i * 2 + b)
                        sp.wait_ge(g_in[p][b], i * 16 * T)
                        load_idx(p, b, i * 2 + b)
            sp.wait_ge(s_fin, 1)
            full = N // P
            sp.dma_start(a["out"][0:full * P, :].rearrange("(q p) f -> p q f", p=P), x[:, 0:full, :]).then_inc(s_out, 16)
            sp.dma_start(a["out"][full * P:N, :], x[0:N - full * P, full, :]).then_inc(s_out, 16)
            sp.wait_ge(s_out, 32)
            sp.wait_ge(s_tab, 16 * 5)

        @block.gpsimd
        def _(pool):
            nc.gpsimd.iota(iota_i[:, :], [[1, NP_]], base=0, channel_multiplier=0).then_inc(s_iota, 1)
            nc.gpsimd.iota(pid_i[:, :], [[0, 1]], base=0, channel_multiplier=1).then_inc(s_iota, 1)
            pool.wait_ge(s_ext, 1)
            nc.gpsimd.partition_all_reduce(extp[:, :, :].rearrange("p a s -> p (a s)"),
                                           ext[:, :, :].rearrange("p a s -> p (a s)"), P, RMAX).then_inc(s_extp, 1)
            pool.sem_inc(ea_lo, 2)
            with pool.Fori(0, PAIRS) as i:
                for b in range(2):
                    pool.wait_ge(ea_cp, i * 2 + b + 1)
                    nc.gpsimd.tensor_tensor(vals[:, b, :, D + 1:2 * D + 1], ea16[:, b, :, :],
                                            vals[:, b, :, 0:D].bitcast(F32), ALU.subtract).then_inc(ea_lo, 1)
            for p in range(5):
                pool.wait_ge(s_tab, 16 * (p + 1))
                with pool.Fori(0, PAIRS) as i:
                    for b in range(2):
                        s = i * 2 + b
                        if p < 2:
                            pool.wait_ge(p_done[p], s * T + 1)
                        elif p == 2:
                            pool.wait_ge(vp_done, s * 3 + 1)
                        else:
                            pool.wait_ge(g_used[p], s + 1)
                        pool.sem_inc(s_zero, 1)
                        pool.wait_ge(idx_in[p][b], (i + 1) * 16)
                        pool.sem_inc(s_zero, 1)
                        for t in range(T):
                            nc.gpsimd.indirect_dma_start(
                                out=gb[:, b, t, 0:tabw[p]], out_offset=None, in_=tabs[p],
                                in_offset=bass.IndirectOffsetOnAxis(ap=idx[:, b, t:t + 1], axis=0)).then_inc(g_in[p][b], 16)

        @block.scalar
        def _(act):
            taken = [0]

            def root(out, in_):
                act.wait_ge(s_sqi, taken[0] + 1)
                nc.scalar.activation(out, in_, ACT.Sqrt).then_inc(s_sqo, 1)
                taken[0] += 1

            def node_root():
                root(r1_root[:, :], r1[:, :])

            def stat_root():
                root(sv_root[:, :], sv[:, 0:D])

            root(rn_root, rn[:, :, :].rearrange("p s t -> p (s t)"))
            with act.Fori(0, PAIRS) as i:
                for b in range(2):
                    act.wait_ge(ea_in[b], (i + 1) * 16)
                    act.wait_ge(row_used[0], i * 2 + b + 1)
                    nc.scalar.activation(vals[:, b, :, 0:D], ea16[:, b, :, :], ACT.Copy).then_inc(ea_cp, 1)
            act.wait_ge(s_par, 16 * 21)
            node_root()
            node_root()
            for l in range(2):
                act.sem_inc(a_done[l], 2)
                with act.Fori(0, PAIRS) as i:
                    for b in range(2):
                        s = i * 2 + b

                        def hidden(c):
                            act.wait_ge(h_mm[l], s * 2 + c + 4)
                            if c == 0:
                                act.wait_ge(w_mm[l], s * T + 1)
                            nc.scalar.activation(ht[0:EK, b, c * 512:(c + 1) * 512], ps[0:EK, 5, :], ACT.Relu,
                                                 bias=b1[l][:, 0:1]).then_inc(h_act[l], 1)

                        def source_onehots(g):
                            if g == 0:
                                act.wait_ge(sc_mm[l], s * T + 1)
                            for t in range(g * 3, g * 3 + 3):
                                nc.scalar.activation(oh5[:, b, t, :], iota_f[:, 0:CW], ACT.Abs,
                                                     bias=src_n[:, bass.ds(s, 1), t]).then_inc(a_abs[l], 1)
                            act.wait_ge(a_abs[l], s * AT + g * 3 + 3)
                            nc.scalar.activation(oh5[:, b, g * 3:g * 3 + 3, :], oh5[:, b, g * 3:g * 3 + 3, :].bitcast(F32),
                                                 ACT.Relu, bias=ones[:, 0:1], scale=-1.0).then_inc(a_done[l], 1)

                        hidden(0)
                        source_onehots(0)
                        hidden(1)
                        source_onehots(1)
                stat_root()
                if l == 0:
                    stat_root()
                else:
                    node_root()
            with act.Fori(0, PAIRS) as i:
                for b in range(2):
                    s = i * 2 + b
                    act.wait_ge(vp_done, s * 3 + 7)
                    act.wait_ge(row_used[1], s + 1)
                    nc.scalar.activation(v96[:, b, :, 0, :], v48[:, b, :, :], ACT.Copy).then_inc(vh_done, 1)
            stat_root()
            node_root()
            for k in range(2):
                act.wait_ge(s_thi, k + 1)
                nc.scalar.activation(hh[:, :, :], t1[:, :, 0:D], ACT.Tanh).then_inc(s_th, 1)
            node_root()

        @block.tensor
        def _(pe):
            def zero_bank(bk):
                return nc.tensor.matmul(ps[:, bk, :], zeros[:, 0:P], zeros[:, :], start=True, stop=False, skip_group_check=True)

            def window_matmuls(w, s, rhs_of, out_of):
                lo, hi, off = load_window(pe, s)
                with pe.Fori(lo, hi) as c:
                    c = nc.s_assert_within(c, 0, NB - 1, skip_runtime_bounds_check_because="a block index out of the window table")
                    for h in range(2):
                        pe.wait_ge(oh_ready[w][h], off + c + 1)
                        for u in range(T // 2):
                            mm = nc.tensor.matmul(out_of(c), (oh_r if w < 2 else oh_b)[:, h, u, :], rhs_of(h * (T // 2) + u),
                                                  start=False, stop=False, skip_group_check=True)
                        mm.then_inc(oh_used[w][h], 1)

            def partition_sum(k):
                pe.wait_ge(s_str, k + 1)
                nc.tensor.matmul(ps[:, 5, 0:32], ones[:, :], stat[:, :], start=True, stop=True,
                                 skip_group_check=True).then_inc(s_sts, 1)

            def node_product(k, rows, wts):
                K = wts.shape[0]
                pe.wait_ge(s_nmi, k + 1)
                for q in range(NB):
                    tr = nc.tensor.transpose(ps[0:K, TBANK[q // 4], (q % 4) * P:(q % 4 + 1) * P], rows(q), ident[:, :])
                tr.then_inc(s_nmt, 1)
                pe.wait_ge(s_nmc, (k + 1) * 7)
                for q in range(NB):
                    mm = nc.tensor.matmul(ps[:, 5, 64 + q * D:64 + (q + 1) * D], xt[0:K, q, :], wts,
                                          start=True, stop=True, skip_group_check=True)
                mm.then_inc(s_nmo, 1)

            pe.wait_ge(s_setup, 1)
            for w in range(4):
                for h in range(2):
                    pe.sem_inc(oh_used[w][h], BIAS + 1)
            for w in range(4):
                pe.sem_inc(row_used[w], 2)
            pe.wait_ge(s_par, 16 * 21)

            for bk in range(4):
                zero_bank(bk)
            with pe.Fori(0, PAIRS) as i:
                for b in range(2):
                    s = i * 2 + b
                    pe.wait_ge(ea_cp, s + 1)
                    pe.wait_ge(ea_lo, s + 3)
                    window_matmuls(0, s, lambda t: vals[:, b, t, :], lambda c: psf[:, bass.ds(c * 64, 2 * (D + 1))])
                    nc.tensor.matmul(ps[:, 6, 0:32], zeros[:, 0:P], zeros[:, 0:32], start=True, stop=True)\
                        .then_inc(row_used[0], 1)
            nc.tensor.matmul(ps[:, 6, 0:32], zeros[:, 0:P], zeros[:, 0:32], start=True, stop=True).then_inc(s_accd, 1)

            for l in range(2):
                W = NH * MP[l]
                pe.wait_ge(s_node, l + 1)
                pe.sem_inc(h_mm[l], 3)
                pe.sem_inc(w_mm[l], 9)
                pe.sem_inc(sc_mm[l], 9)
                for bk in range(5):
                    zero_bank(bk)

                def scatter_tile(b, s1, t):
                    if t % 2 == 0:
                        pe.wait_ge(o_done[l], s1 * 4 + t // 2 + 2)
                    if t % 3 == 0 and t < AT:
                        pe.wait_ge(a_done[l], s1 * 2 + t // 3 + 1)
                    if t == AT:
                        pe.wait_ge(l_done[l], s1 * 3 + 1)
                    for c in range(NC):
                        out = ps[:, c, 0:W] if l == 0 else ps[:, c // 3, (c % 3) * W:(c % 3 + 1) * W]
                        mm = nc.tensor.matmul(out, oh5[:, b, t, c * P:(c + 1) * P], big[:, b, t, 0:W],
                                              start=False, stop=False, skip_group_check=True)
                    mm.then_inc(sc_mm[l], 1)

                with pe.Fori(0, PAIRS) as i:
                    for b in range(2):
                        s = i * 2 + b

                        def hidden(c):
                            pe.wait_ge(h_act[l], s * 2 + c + 1)
                            nc.tensor.matmul(ps[:, 5, :], w1[l][:, :], eat[:, b, c * 512:(c + 1) * 512],
                                             start=True, stop=True).then_inc(h_mm[l], 1)

                        pe.wait_ge(eat_in[l][b], (i + 1) * 16)
                        hidden(0)
                        for t in range(T):
                            if t == 2:
                                hidden(1)
                            if t % 4 == 0:
                                pe.wait_ge(h_act[l], s * 2 + t // 4 + 2)
                            pe.wait_ge(p_done[l], s * T + t + 8)
                            nc.tensor.matmul(ps[:, 6 + t % 2, 0:MJ * D], ht[:, b, t * P:(t + 1) * P],
                                             w2[l][:, :], start=True, stop=True).then_inc(w_mm[l], 1)
                            scatter_tile(1 - b, s, t)
                for t in range(T):
                    scatter_tile(1, NSUP, t)
                nc.tensor.matmul(ps[:, 7, 0:32], zeros[:, 0:P], zeros[:, 0:32], start=True, stop=True).then_inc(s_accd, 1)
                if l == 0:
                    for k in range(3):
                        partition_sum(k)
                else:
                    for k in range(3, 5):
                        partition_sum(k)

            for p in range(2, 5):
                w = p - 1
                pe.wait_ge(s_node, p + 1)
                for bk in range(7 if p == 2 else 4):
                    zero_bank(bk)
                with pe.Fori(0, PAIRS) as i:
                    for b in range(2):
                        s = i * 2 + b
                        if p == 2:
                            pe.wait_ge(vl_done, s + 3)
                            window_matmuls(w, s, lambda t: v96[:, b, t, :, :].rearrange("p k f -> p (k f)"),
                                           lambda c: psf[:, bass.ds(c * 128, 6 * D)])
                        else:
                            pe.wait_ge(g_in[p][b], (i + 1) * 16 * T)
                            window_matmuls(w, s, lambda t: gb[:, b, t, 0:3 * D // 2].bitcast(BF16),
                                           lambda c: psf[:, bass.ds(c * 64, 3 * D)])
                        mm = nc.tensor.matmul(ps[:, 7, 0:32], zeros[:, 0:P], zeros[:, 0:32], start=True, stop=True)
                        mm.then_inc(row_used[w] if p == 2 else g_used[p], 1)
                nc.tensor.matmul(ps[:, 7, 0:32], zeros[:, 0:P], zeros[:, 0:32], start=True, stop=True).then_inc(s_accd, 1)
                if p == 2:
                    node_product(0, lambda q: acc[:, q, :], wst[:, :])
                    for k in range(5, 7):
                        partition_sum(k)
                    node_product(1, lambda q: x[:, q, :], gw1[:, :])
                if p == 3:
                    node_product(2, lambda q: hh[:, q, :], gw2[:, :])

        @block.vector
        def _(dve):
            V = nc.vector
            chain = [0]

            def link(ins):
                chain[0] += 1
                ins.then_inc(s_dve, 1)
                dve.wait_ge(s_dve, chain[0])

            def bc(ap, n):
                return repeat(ap, len(ap.shape), n)

            roots = [2]

            def square_root(v, root, tmp, k):
                dve.wait_ge(s_sqo, k)
                link(V.tensor_scalar(tmp, root, 1e-30, None, ALU.max))
                link(V.reciprocal(tmp, tmp))
                link(V.tensor_tensor(tmp, tmp, v, ALU.mult))
                link(V.tensor_tensor(root, root, tmp, ALU.add))
                link(V.tensor_scalar(root, root, 0.5, None, ALU.mult))

            link(V.memset(zeros[:, :], 0.0))
            link(V.memset(ones[:, :], 1.0))
            link(V.memset(vals[:, :, :, D:D + 1].bitcast(F32), 1.0))
            link(V.memset(vals[:, :, :, 2 * D + 1:2 * D + 2].bitcast(F32), 0.0))
            link(V.memset(parts[0][:, :, :, MF:MF + 1].bitcast(F32), 1.0))
            link(V.memset(parts[0][:, :, :, 2 * MF + 1:2 * MF + 2].bitcast(F32), 0.0))
            link(V.memset(eat[:, :, :], 0.0))
            link(V.memset(ht[:, :, :], 1.0))
            for l in range(2):
                link(V.memset(w1[l][:, :], 0.0))
                link(V.memset(w2[l][:, :], 0.0))
            dve.sem_inc(s_pad, 1)
            link(V.memset(stat[:, :], 0.0))
            dve.wait_ge(s_iota, 2)
            link(V.tensor_copy(iota_f[:, :], iota_i[:, :]))
            link(V.tensor_copy(pid_f[:, :], pid_i[:, :]))
            link(V.tensor_scalar(ident[:, :], iota_f[:, 0:P], pid_f[:, 0:1], None, ALU.is_equal))
            link(V.tensor_scalar(node_id[:, :], iota_f[:, 0:NB], float(P), pid_f[:, 0:1], ALU.mult, ALU.add))
            link(V.tensor_scalar(mask[:, :], node_id[:, :], float(N), None, ALU.is_lt))
            dve.wait_ge(s_idx0, 64)
            link(V.tensor_copy(dst_f[:, :, :], dst_i[:, :, :]))
            link(V.tensor_scalar(neg_dst[:, :, :], dst_f[:, :, :], -1.0, None, ALU.mult))
            link(V.tensor_reduce(ext[:, 0, :], dst_f[:, :, :], AX.X, ALU.max))
            V.tensor_reduce(ext[:, 1, :], neg_dst[:, :, :], AX.X, ALU.max).then_inc(s_ext, 1)
            link(V.tensor_copy(src_f[:, :, :], src_i[:, :, :]))
            link(V.tensor_scalar(src_h[:, :, :], src_f[:, :, :], float(CW), None, ALU.is_ge))
            for k in range(2, NH):
                link(V.scalar_tensor_tensor(out=src_h[:, :, :], in0=src_f[:, :, :], scalar=float(k * CW),
                                            in1=src_h[:, :, :], op0=ALU.is_ge, op1=ALU.add))
            link(V.scalar_tensor_tensor(out=src_v[:, :, :], in0=src_h[:, :, :], scalar=-float(CW),
                                        in1=src_f[:, :, :], op0=ALU.mult, op1=ALU.add))
            link(V.tensor_scalar(src_n[:, :, :], src_v[:, :, :], -1.0, None, ALU.mult))
            dve.wait_ge(s_extp, 1)
            link(V.tensor_copy(ext_i[:, 0, :], extp[:, 0, :]))
            link(V.tensor_scalar(ext_i[:, 1, :], extp[:, 1, :], -1.0, None, ALU.mult))
            link(V.tensor_scalar(blk_i[:, :, :], ext_i[:, :, :], 7, None, ALU.logical_shift_right))
            link(V.tensor_copy(blk[:, :, :], blk_i[:, :, :]))
            link(V.tensor_tensor(cnt_w[:, :], blk[:, 0, :], blk[:, 1, :], ALU.subtract))
            link(V.tensor_scalar(cnt_w[:, :], cnt_w[:, :], 1.0, None, ALU.add))
            link(V.tensor_tensor_scan(cum_w[:, :], ones[:, 0:NSUP], cnt_w[:, :], 0.0, ALU.mult, ALU.add))
            link(V.tensor_tensor(cum_w[:, :], cum_w[:, :], cnt_w[:, :], ALU.subtract))
            link(V.tensor_tensor(cum_w[:, :], cum_w[:, :], blk[:, 1, :], ALU.subtract))
            link(V.tensor_scalar(win_f[:, :], blk[:, 0, :], 32.0, 32.0 + 1024.0 * BIAS, ALU.mult, ALU.add))
            link(V.tensor_tensor(win_f[:, :], win_f[:, :], blk[:, 1, :], ALU.add))
            link(V.tensor_scalar(cum_w[:, :], cum_w[:, :], 1024.0, None, ALU.mult))
            link(V.tensor_tensor(win_f[:, :], win_f[:, :], cum_w[:, :], ALU.add))
            link(V.tensor_copy(win[:, :], win_f[:, :]))
            for w in range(4):
                for h in range(2):
                    dve.sem_inc(oh_ready[w][h], BIAS)
            link(V.memset(sv[:, :], 1.0))
            V.memset(sm[:, :], 0.0).then_inc(s_setup, 1)

            rv = rhat[:, :, :, :].rearrange("p s t c -> p (s t) c")
            rnf = rn[:, :, :].rearrange("p s t -> p (s t)")
            rq = rsq.rearrange("p (n c) -> p n c", c=3)
            link(V.tensor_tensor(rq, rv, rv, ALU.mult))
            V.tensor_reduce(rnf, rq, AX.X, ALU.add).then_inc(s_sqi, 1)
            square_root(rnf, rn_root, rn_t, 1)
            link(V.tensor_scalar(rnf, rn_root, 1e-12, None, ALU.add))
            link(V.reciprocal(rnf, rnf))
            link(V.tensor_tensor(rv, rv, bc(rnf, 3), ALU.mult))

            def window_onehots(w, s):
                lo, hi, off = load_window(dve, s)
                with dve.Fori(lo, hi) as c:
                    c = nc.s_assert_within(c, 0, NB - 1, skip_runtime_bounds_check_because="a block index out of the window table")
                    for h in range(2):
                        dve.wait_ge(oh_used[w][h], off + c + 1)
                        d = dst_f[:, bass.ds(s, 1), h * 4:h * 4 + 4].rearrange("p o t -> p (o t)")
                        cols = repeat(iota_f[:, bass.ds(c * P, P)], 1, T // 2)
                        V.tensor_tensor((oh_r if w < 2 else oh_b)[:, h, :, :], bc(d, P), cols, ALU.is_equal).then_inc(oh_ready[w][h], 1)

            def one_sup(ap3, s):
                return ap3[:, bass.ds(s, 1), :].rearrange("p o t -> p (o t)")

            with dve.Fori(0, PAIRS) as i:
                for b in range(2):
                    s = i * 2 + b
                    window_onehots(0, s)

            def layer_norm(xx):
                link(V.tensor_reduce(r1[:, :], xx, AX.X, ALU.add))
                link(V.tensor_scalar(r1[:, :], r1[:, :], 1.0 / D, None, ALU.mult))
                link(V.tensor_tensor(xx, xx, bc(r1[:, :], D), ALU.subtract))
                link(V.tensor_tensor(t2[:, :, 0:D], xx, xx, ALU.mult))
                link(V.tensor_reduce(r1[:, :], t2[:, :, 0:D], AX.X, ALU.add))
                roots[0] += 1
                V.tensor_scalar(r1[:, :], r1[:, :], 1.0 / D, EPS, ALU.mult, ALU.add).then_inc(s_sqi, 1)
                square_root(r1[:, :], r1_root[:, :], r1_t[:, :], roots[0])
                link(V.reciprocal(r1[:, :], r1_root[:, :]))
                link(V.tensor_tensor(xx, xx, bc(r1[:, :], D), ALU.mult))

            def clear_scatter():
                link(V.memset(big[:, 1, :, :].bitcast(F32), 0.0))
                link(V.memset(oh5[:, 1, :, :].bitcast(F32), 0.0))

            stats = [0]

            def node_sum(src, n):
                V.tensor_reduce(stat[:, 0:n], src.rearrange("p q f -> p f q"), AX.X, ALU.add).then_inc(s_str, 1)
                stats[0] += 1
                dve.wait_ge(s_sts, stats[0])

            def over_nodes(ap, f):
                return repeat(ap, 1, NB)

            def batch_norm(xx, g, b_):
                node_sum(xx, D)
                link(V.tensor_scalar(sm[:, 0:D], ps[:, 5, 0:D], 1.0 / N, None, ALU.mult))
                link(V.tensor_tensor(xx, xx, over_nodes(sm[:, 0:D], D), ALU.subtract))
                link(V.tensor_tensor(xx, xx, bc(mask[:, :], D), ALU.mult))
                link(V.tensor_tensor(t2[:, :, 0:D], xx, xx, ALU.mult))
                node_sum(t2[:, :, 0:D], D)
                roots[0] += 1
                V.tensor_scalar(sv[:, 0:D], ps[:, 5, 0:D], 1.0 / N, EPS, ALU.mult, ALU.add).then_inc(s_sqi, 1)
                square_root(sv[:, 0:D], sv_root[:, :], sv_t[:, :], roots[0])
                link(V.reciprocal(sv[:, 0:D], sv_root[:, :]))
                link(V.tensor_tensor(sv[:, 0:D], sv[:, 0:D], par[:, g, :], ALU.mult))
                link(V.tensor_tensor(xx, xx, over_nodes(sv[:, 0:D], D), ALU.mult))
                link(V.tensor_tensor(xx, xx, over_nodes(par[:, b_, :], D), ALU.add))

            dve.wait_ge(s_accd, 1)
            dve.wait_ge(s_x, 16)
            dve.wait_ge(s_par, 16 * 21)
            a0 = psf[:, 0:NB * 64].rearrange("p (q f) -> p q f", f=64)
            V.tensor_scalar(r1[:, :], a0[:, :, D], 1.0, None, ALU.add).then_inc(s_sqi, 1)
            square_root(r1[:, :], r1_root[:, :], r1_t[:, :], 2)
            link(V.reciprocal(dinv[:, :], r1_root[:, :]))
            link(V.tensor_scalar(rcd[:, :], a0[:, :, D], 1.0, None, ALU.max))
            link(V.reciprocal(rcd[:, :], rcd[:, :]))
            link(V.tensor_copy(t1[:, :, 0:D], a0[:, :, 0:D]))
            link(V.tensor_tensor(t1[:, :, 0:D], t1[:, :, 0:D], a0[:, :, D + 1:2 * D + 1], ALU.add))
            link(V.tensor_tensor(t1[:, :, 0:D], t1[:, :, 0:D], bc(rcd[:, :], D), ALU.mult))
            link(V.tensor_tensor(x[:, :, :], x[:, :, :], t1[:, :, 0:D], ALU.add))
            layer_norm(x[:, :, :])
            V.tensor_copy(tab[:, :, 0:D], x[:, :, :]).then_inc(s_tabr, 1)
            clear_scatter()
            dve.sem_inc(s_node, 1)

            for l in range(2):
                p = l
                dve.sem_inc(h_act[l], 1)
                dve.sem_inc(p_done[l], 9)
                dve.sem_inc(r_done[l], 2)
                dve.sem_inc(o_done[l], 5)
                dve.sem_inc(m_lo[l], 2)
                dve.sem_inc(l_done[l], 1)
                W = MF if l == 0 else D
                L = W + 1 if l == 0 else W
                I_, J_ = (D, MJ) if l == 0 else (MJ, D)
                with dve.Fori(0, PAIRS) as i:
                    for b in range(2):
                        s = i * 2 + b
                        rh = rhat[:, bass.ds(s, 1), :, :].rearrange("p o t c -> p (o t) c")
                        dve.wait_ge(g_in[p][b], (i + 1) * 16 * T)
                        if l == 1:
                            V.tensor_tensor(vprod[:, :, :, :], gb[:, b, :, 0:12].rearrange("p t (j c) -> p t j c", c=3),
                                            repeat(rh, 2, NV), ALU.mult).then_inc(q_done[l], 1)
                            dve.wait_ge(q_done[l], s * 2 + 1)
                            V.tensor_reduce(gb[:, b, :, 28:32], vprod[:, :, :, :], AX.X, ALU.add).then_inc(q_done[l], 1)
                            dve.wait_ge(q_done[l], s * 2 + 2)

                        def reduce_pair(g):
                            pv = prod[:, (2 * g) % 4:(2 * g) % 4 + 2, :].rearrange("p t (i j) -> p t i j", j=J_)
                            dve.wait_ge(p_done[l], s * T + 2 * g + 11)
                            if g == 0:
                                dve.wait_ge(m_lo[l], s + 1)
                            V.tensor_reduce(msg[:, b, 2 * g:2 * g + 2, 0:J_], pv.rearrange("p t i j -> p t j i"),
                                            AX.X, ALU.add).then_inc(r_done[l], 1)

                        for t in range(T):
                            dve.wait_ge(w_mm[l], s * T + t + 10)
                            if t % 2 == 0:
                                dve.wait_ge(r_done[l], s * 4 + t // 2 + 1)
                            xin = gb[:, b, t, 0:D] if l == 0 else gb[:, b, t, 12:32]
                            wv = ps[:, 6 + t % 2, 0:MJ * D].rearrange("p (i j) -> p i j", j=J_)
                            pv = prod[:, t % 4, :].rearrange("p (i j) -> p i j", j=J_)
                            V.tensor_tensor(pv, wv, bc(xin, J_), ALU.mult).then_inc(p_done[l], 1)
                            if t % 2 == 0 and t > 0:
                                reduce_pair(t // 2 - 1)
                        dve.wait_ge(o_done[l], s * 4 + 1)
                        hs = src_h[:, bass.ds(s, 1), :].rearrange("p o t -> p (o t)")
                        V.tensor_tensor(oh_h[:, b, :, :], bc(hs, NH), repeat(iota_f[:, 0:NH], 1, T),
                                        ALU.is_equal).then_inc(l_done[l], 1)
                        reduce_pair(3)
                        dve.wait_ge(sc_mm[l], s * T + 1)
                        for t in range(AT, T):
                            V.tensor_scalar(oh5[:, b, t, :], iota_f[:, 0:CW], src_v[:, bass.ds(s, 1), t], None,
                                            ALU.is_equal).then_inc(l_done[l], 1)
                        dve.wait_ge(r_done[l], s * 4 + 6)
                        if l == 0:
                            V.tensor_tensor(msg[:, b, :, MJ:MJ + 12].rearrange("p t (j c) -> p t j c", c=3),
                                            bc(msg[:, b, :, 0:NV], 3), repeat(rh, 2, NV),
                                            ALU.mult).then_inc(q_done[l], 1)
                            dve.wait_ge(q_done[l], s + 1)
                        m0 = NV if l == 0 else 0
                        V.tensor_copy(parts[l][:, b, :, 0:W], msg[:, b, :, m0:m0 + W]).then_inc(m_hi[l], 1)
                        dve.wait_ge(m_hi[l], s + 1)
                        V.tensor_tensor(parts[l][:, b, :, L:L + W], msg[:, b, :, m0:m0 + W],
                                        parts[l][:, b, :, 0:W].bitcast(F32), ALU.subtract).then_inc(m_lo[l], 1)
                        dve.wait_ge(l_done[l], s * 3 + 2)
                        dve.wait_ge(m_lo[l], s + 3)
                        for g in range(4):
                            V.tensor_tensor(big[:, b, 2 * g:2 * g + 2, 0:NH * MP[l]].rearrange("p t (h f) -> p t h f", h=NH),
                                            repeat(parts[l][:, b, 2 * g:2 * g + 2, :].bitcast(F32), 2, NH),
                                            bc(oh_h[:, b, 2 * g:2 * g + 2, :], MP[l]), ALU.mult).then_inc(o_done[l], 1)
                dve.wait_ge(s_accd, l + 2)
                if l == 0:
                    t1c = t1[:, :, :].rearrange("p (h c) f -> p h c f", c=NC)
                    rcc = rcs[:, :].rearrange("p (h c) -> p h c", c=NC)
                    for c in range(NC):
                        av = ps[:, c, 0:NH * MP[0]].rearrange("p (h f) -> p h f", h=NH)
                        link(V.tensor_scalar(rcc[:, :, c], av[:, :, MF], 1.0, None, ALU.max))
                        link(V.tensor_copy(t1c[:, :, c, 0:MF], av[:, :, 0:MF]))
                        link(V.tensor_tensor(t1c[:, :, c, 0:MF], t1c[:, :, c, 0:MF], av[:, :, MF + 1:2 * MF + 1], ALU.add))
                    link(V.reciprocal(rcs[:, :], rcs[:, :]))
                    link(V.tensor_tensor(rcs[:, :], rcs[:, :], mask[:, :], ALU.mult))
                    link(V.tensor_tensor(t1[:, :, 0:MF], t1[:, :, 0:MF], bc(rcs[:, :], MF), ALU.mult))
                    link(V.tensor_scalar(tab[:, :, 12:MF], t1[:, :, 0:D], 0.25, None, ALU.mult))
                    link(V.tensor_scalar(tab[:, :, 0:12], t1[:, :, D:MF], 0.25 * 3.0 ** 0.5, None, ALU.mult))
                    batch_norm(tab[:, :, 12:MF], GS0, BS0)
                    link(V.tensor_tensor(t2[:, :, 0:12], tab[:, :, 0:12], tab[:, :, 0:12], ALU.mult))
                    node_sum(t2[:, :, 0:12], 12)
                    link(V.tensor_copy(sm[:, 0:12], ps[:, 5, 0:12]))
                    link(V.tensor_reduce(sv[:, 0:NV], sm[:, 0:12].rearrange("p (j c) -> p j c", c=3), AX.X, ALU.add))
                    roots[0] += 1
                    V.tensor_scalar(sv[:, 0:D], sv[:, 0:D], 1.0 / (3 * N), EPS, ALU.mult, ALU.add).then_inc(s_sqi, 1)
                    square_root(sv[:, 0:D], sv_root[:, :], sv_t[:, :], roots[0])
                    link(V.reciprocal(sv[:, 0:D], sv_root[:, :]))
                    link(V.tensor_tensor(sv[:, 0:NV], sv[:, 0:NV], par[:, GV0, 0:NV], ALU.mult))
                    link(V.tensor_copy(sm[:, 0:12].rearrange("p (j c) -> p j c", c=3), bc(sv[:, 0:NV], 3)))
                    V.tensor_tensor(tab[:, :, 0:12], tab[:, :, 0:12], over_nodes(sm[:, 0:12], 12), ALU.mult).then_inc(s_tabr, 1)
                    clear_scatter()
                    dve.sem_inc(s_node, 1)
                else:
                    t1c = t1[:, :, :].rearrange("p (h c) f -> p h c f", c=NC)
                    for c in range(NC):
                        W5 = NH * MP[1]
                        av = ps[:, c // 3, (c % 3) * W5:(c % 3 + 1) * W5].rearrange("p (h f) -> p h f", h=NH)
                        link(V.tensor_copy(t1c[:, :, c, 0:D], av[:, :, 0:D]))
                        link(V.tensor_tensor(t1c[:, :, c, 0:D], t1c[:, :, c, 0:D], av[:, :, D:2 * D], ALU.add))
                    link(V.tensor_tensor(t1[:, :, 0:D], t1[:, :, 0:D], bc(rcs[:, :], D), ALU.mult))
                    link(V.tensor_scalar(t1[:, :, 0:D], t1[:, :, 0:D], float(MJ) ** -0.5, None, ALU.mult))
                    batch_norm(t1[:, :, 0:D], GS1, BS1)
                    link(V.tensor_tensor(x[:, :, :], x[:, :, :], t1[:, :, 0:D], ALU.add))
                    layer_norm(x[:, :, :])
                    dve.wait_ge(s_tab, 32)
                    V.tensor_copy(tab[:, :, 0:D], x[:, :, :]).then_inc(s_tabr, 1)
                    dve.sem_inc(s_node, 1)

            products = [0]

            def node_product(K):
                k = products[0]
                products[0] += 1
                dve.wait_ge(s_nmt, k + 1)
                for j in range(7):
                    n = min(4, NB - 4 * j)
                    V.tensor_copy(xt[0:K, 4 * j:4 * j + n, :],
                                  ps[0:K, TBANK[j], 0:n * P].rearrange("k (n c) -> k n c", c=P)).then_inc(s_nmc, 1)
                dve.wait_ge(s_nmo, k + 1)
                return ps[:, 5, 64:64 + NB * D].rearrange("p (q f) -> p q f", f=D)

            def scaled_table(res):
                link(V.tensor_tensor(tab[:, :, 0:D], res, bc(dinv[:, :], D), ALU.mult))
                link(V.tensor_copy(tabb[:, :, 0, :], tab[:, :, 0:D]))
                link(V.tensor_tensor(t2[:, :, 0:D], tab[:, :, 0:D], tabb[:, :, 0, :], ALU.subtract))
                link(V.tensor_copy(tabb[:, :, 1, :], t2[:, :, 0:D]))
                link(V.tensor_tensor(t2[:, :, 0:D], t2[:, :, 0:D], tabb[:, :, 1, :], ALU.subtract))
                chain[0] += 1
                V.tensor_copy(tabb[:, :, 2, :], t2[:, :, 0:D]).then_inc(s_dve, 1)
                dve.wait_ge(s_dve, chain[0])
                dve.sem_inc(s_tabr, 1)

            for p in range(2, 5):
                w = p - 1
                if p == 2:
                    dve.sem_inc(vp_done, 4)
                    dve.sem_inc(vl_done, 2)
                else:
                    dve.sem_inc(g_used[p], 2)
                with dve.Fori(0, PAIRS) as i:
                    for b in range(2):
                        s = i * 2 + b
                        if p == 2:
                            dve.wait_ge(g_in[p][b], (i + 1) * 16 * T)
                            dve.wait_ge(vl_done, s + 1)
                            for k in range(2):
                                ek = ea2[:, bass.ds(s, 1), :, k].rearrange("p o t -> p (o t)")
                                V.tensor_tensor(v48[:, b, :, k * D:(k + 1) * D], gb[:, b, :, 0:D], bc(ek, D),
                                                ALU.mult).then_inc(vp_done, 1)
                            V.tensor_copy(v48[:, b, :, 2 * D:3 * D], gb[:, b, :, 0:D]).then_inc(vp_done, 1)
                            dve.wait_ge(vp_done, s * 3 + 7)
                            dve.wait_ge(vh_done, s + 1)
                            V.tensor_tensor(v96[:, b, :, 1, :], v48[:, b, :, :], v96[:, b, :, 0, :].bitcast(F32),
                                            ALU.subtract).then_inc(vl_done, 1)
                        window_onehots(w, s)
                dve.wait_ge(s_accd, p + 2)
                if p == 2:
                    av = psf[:, 0:NB * 128].rearrange("p (q f) -> p q f", f=128)
                    link(V.tensor_copy(acc[:, :, 0:3 * D], av[:, :, 0:3 * D]))
                    link(V.tensor_tensor(acc[:, :, 0:3 * D], acc[:, :, 0:3 * D], av[:, :, 3 * D:6 * D], ALU.add))
                    link(V.tensor_tensor(acc[:, :, 0:3 * D], acc[:, :, 0:3 * D], bc(rcd[:, :], 3 * D), ALU.mult))
                    V.tensor_copy(acc[:, :, 3 * D:4 * D], x[:, :, :]).then_inc(s_nmi, 1)
                    res = node_product(4 * D)
                    link(V.tensor_tensor(t1[:, :, 0:D], res, over_nodes(par[:, B2, :], D), ALU.add))
                    link(V.tensor_tensor(t1[:, :, 0:D], t1[:, :, 0:D], bc(mask[:, :], D), ALU.mult))
                    batch_norm(t1[:, :, 0:D], GA, BE)
                    link(V.scalar_tensor_tensor(out=t2[:, :, 0:D], in0=t1[:, :, 0:D], scalar=0.01, in1=t1[:, :, 0:D],
                                                op0=ALU.mult, op1=ALU.max))
                    link(V.tensor_tensor(t2[:, :, 0:D], t2[:, :, 0:D], x[:, :, :], ALU.add))
                    link(V.tensor_tensor(x[:, :, :], t2[:, :, 0:D], x[:, :, :], ALU.add))
                    layer_norm(x[:, :, :])
                    dve.sem_inc(s_nmi, 1)
                    res = node_product(D)
                    dve.wait_ge(s_tab, 48)
                    scaled_table(res)
                    dve.sem_inc(s_node, 1)
                else:
                    av = psf[:, 0:NB * 64].rearrange("p (q f) -> p q f", f=64)
                    link(V.tensor_tensor(t2[:, :, 0:D], av[:, :, 2 * D:3 * D], tab[:, :, 0:D], ALU.add))
                    link(V.tensor_tensor(t2[:, :, 0:D], t2[:, :, 0:D], av[:, :, D:2 * D], ALU.add))
                    link(V.tensor_tensor(t2[:, :, 0:D], t2[:, :, 0:D], av[:, :, 0:D], ALU.add))
                    link(V.tensor_tensor(t2[:, :, 0:D], t2[:, :, 0:D], bc(dinv[:, :], D), ALU.mult))
                    V.tensor_tensor(t1[:, :, 0:D], t2[:, :, 0:D],
                                    over_nodes(par[:, C1, :] if p == 3 else c2[:, :], D), ALU.add).then_inc(s_thi, 1)
                    dve.wait_ge(s_th, p - 2)
                    if p == 3:
                        dve.sem_inc(s_nmi, 1)
                        res = node_product(D)
                        dve.wait_ge(s_tab, 64)
                        scaled_table(res)
                        dve.sem_inc(s_node, 1)
                    else:
                        link(V.tensor_tensor(x[:, :, :], x[:, :, :], hh[:, :, :], ALU.add))
                        layer_norm(x[:, :, :])
                        dve.sem_inc(s_fin, 1)


def kernel(**inputs):
    import numpy as np
    import concourse.bacc as bacc
    from concourse import mybir as mb
    from concourse.bass_utils import run_bass_kernel_spmd as run

    g = {k: np.asarray(v) for k, v in inputs.items()}

    def pad_rows(v, n, fill=0):
        out = np.full((n,) + v.shape[1:], fill, v.dtype)
        out[:v.shape[0]] = v
        return out

    arrays = {
        "x": pad_rows(g["x"], NP_),
        "src": pad_rows(g["src"], EP, DUMP),
        "dst": pad_rows(g["dst"], EP, DUMP),
        "edge_attr_2": pad_rows(g["edge_attr_2"], EP),
        "edge_attr_3": pad_rows(g["edge_attr_3"], EP),
        "edge_attr_16": pad_rows(g["edge_attr_16"], EP),
        "eat": pad_rows(g["edge_attr_48"], EP).reshape(NSUP, P, T, EK).transpose(0, 3, 2, 1).reshape(NSUP, EK, SUP),
    }
    for l in range(2):
        w2 = np.concatenate([g[f"L1_gnn_fc{l}_w2"], g[f"L1_gnn_fc{l}_b2"][None]], axis=0)
        if l == 0:
            wa = w2[:, :D * D].reshape(EK + 1, D, D)
            wb = w2[:, D * D:].reshape(EK + 1, D, NV)
            w2 = np.concatenate([wb, wa], axis=2).reshape(EK + 1, D * MJ)
        arrays[f"w2_{l}"] = w2
        w1 = np.zeros((EK, P), np.float32)
        w1[:, :EK] = g[f"L1_gnn_fc{l}_w1"]
        arrays[f"w1_{l}"] = w1
        arrays[f"b1_{l}"] = g[f"L1_gnn_fc{l}_b1"]
    arrays["w_enet"] = g["L2_gnn_W_enet"].reshape(2 * D, D)
    arrays["b_enet"] = g["L2_gnn_b_enet"].reshape(D, D)
    arrays["w_root"] = g["L2_gnn_W_root"]
    arrays["gw1"] = g["L3_gnn_W1"]
    arrays["gw2"] = g["L3_gnn_W2"]
    for short, full in (("gs0", "L1_gnn_bn0_gs"), ("bs0", "L1_gnn_bn0_bs"), ("gv0", "L1_gnn_bn0_gv"),
                        ("gs1", "L1_gnn_bn1_gs"), ("bs1", "L1_gnn_bn1_bs"), ("bias", "L2_gnn_bias"),
                        ("gamma", "L2_gnn_gamma"), ("beta", "L2_gnn_beta"), ("gb1", "L3_gnn_b1"), ("gb2", "L3_gnn_b2")):
        arrays[short] = g[full]
    nc = bacc.Bacc("TRN2", target_bir_lowering=False, num_devices=1)
    feeds, aps = {}, {}
    for name, v in arrays.items():
        v = np.ascontiguousarray(v)
        feeds[f"in_{name}"] = v
        aps[name] = nc.dram_tensor(f"in_{name}", v.shape, mb.dt.from_np(v.dtype), kind="ExternalInput").ap()
    aps["out"] = nc.dram_tensor("out_x", (N, D), mb.dt.float32, kind="ExternalOutput").ap()
    build(nc, aps)
    r = run(nc, [feeds], core_ids=[0])
    return r.results[0]["out_x"]
```

```python
from contextlib import ExitStack

import concourse.bass as bass
from concourse import mybir

ALU = mybir.AluOpType
ACT = mybir.ActivationFunctionType
AX = mybir.AxisListType
F32 = mybir.dt.float32
BF16 = mybir.dt.bfloat16
F16 = mybir.dt.float16
I32 = mybir.dt.int32
F32R = mybir.dt.float32r
RMAX = bass.bass_isa.ReduceOp.max

P = 128
N = 3125
E = 100000
D = 16
NB = -(-N // P)
NP_ = NB * P
T = 8
SUP = T * P
NSUP = 98
EP = NSUP * SUP
PAIRS = NSUP // 2
EK = 48
NV = 4
MJ = D + NV
MF = D + 3 * NV
EPS = 1e-5
DUMP = NP_ - 1
NC = 5
NH = NB // NC
CW = NC * P
AT = 7
LAG = 3
WBANKS = [[6, 7], [2, 3, 6, 7]]
MP = [2 * (MF + 1), 2 * D]
QUADS = PAIRS // 2
GW = NH * 3 * D
AW = NH * D
ABANK = 512 // AW
EW = 6 * D
EBANK = 512 // EW
BIAS = NB - 1
assert PAIRS % 2 == 1 and NSUP % 2 == 0 and EP >= E and NP_ > N


def repeat(ap, axis, n):
    wide = ap.unsqueeze(axis)
    shape = list(wide.shape)
    shape[axis] = n
    return wide.broadcast_to(shape)


def build(nc, a):
    with ExitStack() as ctx:
        def sb(name, shape, dt=F32):
            return ctx.enter_context(nc.sbuf_tensor(name, shape, dt))

        def sem(name):
            return ctx.enter_context(nc.semaphore(name))

        with nc.sbuf_tensor("big", [P, 2, T, NH * MP[0]], F32R) as big, nc.sbuf_tensor("oh5", [P, 2, T, CW], F32R) as oh5:
            pass
        oht = sb("oht", [P, 2, NC, SUP], BF16)
        mk = sb("mk", [P, 2, T, GW], BF16)
        mkf = mk[:, :, :, :].rearrange("p b t n -> p b (t n)").bitcast(F32)[:, :, 0:T * AW]\
            .rearrange("p b (t n) -> p b t n", t=T)
        sb("rest", [P, 2 * T * (NH * MP[0] + CW) - NC * SUP - T * GW])
        dst_i = sb("dst_i", [P, NSUP, T], I32)
        dst_f = sb("dst_f", [P, NSUP, T])
        src_i = sb("src_i", [P, NSUP, T], I32)
        src_f = sb("src_f", [P, NSUP, T])
        src_h = sb("src_h", [P, NSUP, T])
        src_v = sb("src_v", [P, NSUP, T])
        src_n = sb("src_n", [P, NSUP, T])
        rhat = sb("rhat", [P, NSUP, T, 3])
        rn = sb("rn", [P, NSUP, T])
        ea2 = sb("ea2", [P, NSUP, T, 2])
        xt = sb("xt", [P, NB, P])
        xtf = xt[:, :, :].rearrange("p q c -> p (q c)")
        iota_i = xtf.bitcast(I32)
        rsq = xtf[:, 0:NSUP * T * 3]
        iota_f = sb("iota_f", [P, NP_])
        pid_i = sb("pid_i", [P, 1], I32)
        pid_f = sb("pid_f", [P, 1])
        ident = sb("ident", [P, P])
        ones = sb("ones", [P, P])
        zeros = sb("zeros", [P, 512], BF16)
        mask = sb("mask", [P, NB])
        node_id = sb("node_id", [P, NB])
        ext = sb("ext", [P, 2, NSUP])
        extp = sb("extp", [P, 2, NSUP])
        ext_i = sb("ext_i", [P, 2, NSUP], I32)
        blk_i = sb("blk_i", [P, 2, NSUP], I32)
        blk = sb("blk", [P, 2, NSUP])
        cnt_w = sb("cnt_w", [P, NSUP])
        cum_w = sb("cum_w", [P, NSUP])
        win_f = sb("win_f", [P, NSUP])
        blk2 = sb("blk2", [P, 2, PAIRS])
        win2 = sb("win2", [P, PAIRS], I32)
        win = sb("win", [P, NSUP], I32)
        neg_dst = rn

        ea16 = sb("ea16", [P, 2, T, D])
        vals = sb("vals", [P, 4, T, 2 * (D + 1)], F32R)
        oh_r = oh5[:, 1, :, :].rearrange("p t n -> p (t n)")[:, 0:2 * SUP]\
            .rearrange("p (b t n) -> p b t n", b=2, t=T)
        oh_b = sb("oh_b", [P, 2, T // 2, P], BF16)
        oh_h = sb("oh_h", [P, 2, T, NH])
        eat = sb("eat", [P, 2, SUP])
        ht = sb("ht", [P, 2, SUP])
        idx = sb("idx", [P, 2, T], I32)
        gb = sb("gb", [P, 2, T, 32])
        vb = eat[:, :, 0:SUP // 2].bitcast(F16)
        pid_c = sb("pid_c", [P, NC])
        vprod = sb("vprod", [P, T, NV, 3])
        prod = sb("prod", [P, 4, MJ * D])
        msg = sb("msg", [P, 2, T, 32])
        parts = [sb(f"parts{l}", [P, 2, T, MP[l]], F32R) for l in range(2)]
        gx = gb[:, :, :, D:2 * D]
        v48 = sb("v48", [P, 2, T, 3 * D])
        v96 = sb("v96", [P, 2, T, 2, 3 * D], F32R)
        tabb = sb("tabb", [P, NB, 3, D], BF16)
        w1 = [sb(f"w1_{l}", [P, P]) for l in range(2)]
        b1 = [sb(f"b1_{l}", [EK, 1]) for l in range(2)]
        w2 = [sb(f"w2_{l}", [P, MJ * D]) for l in range(2)]
        par = sb("par", [P, 9, D])
        GS0, BS0, GV0, GS1, BS1, B2, GA, BE, C1 = range(9)
        c2 = sb("c2", [P, D])
        wst = sb("wst", [4 * D, D])
        gw1 = sb("gw1", [D, D])
        gw2 = sb("gw2", [D, D])

        x = sb("x", [P, NB, D])
        acc = sb("acc", [P, NB, 64])
        accf = acc[0:NSUP, :, :].rearrange("p q f -> p (q f)")
        row_i = accf[:, 0:SUP].bitcast(I32)
        row_v = accf[:, SUP:SUP + SUP // 2].bitcast(F16)
        row_f = ht[0:NSUP, 0, :]
        row_h = ht[0:NSUP, 1, :]
        t1 = sb("t1", [P, NB, 32])
        t2 = sb("t2", [P, NB, 32])
        r1 = sb("r1", [P, NB])
        rcd = sb("rcd", [P, NB])
        rcs = sb("rcs", [P, NB])
        dinv = sb("dinv", [P, NB])
        tab = sb("tab", [P, NB, 32])
        hh = sb("hh", [P, NB, D])
        stat = sb("stat", [P, 32])
        sm = sb("sm", [P, 32])
        sv = sb("sv", [P, 32])
        r1_root = sb("r1_root", [P, NB])
        r1_t = sb("r1_t", [P, NB])
        sv_root = sb("sv_root", [P, D])
        sv_t = sb("sv_t", [P, D])
        rn_root = xtf[:, 0:NSUP * T]
        rn_t = xtf[:, NSUP * T:2 * NSUP * T]

        ps = ctx.enter_context(nc.psum_tensor("ps", [P, 8, 512], F32))
        psf = ps[:, :, :].rearrange("p b n -> p (b n)")
        TBANK = [0, 1, 2, 3, 4, 6, 7]

        s_par = sem("s_par")
        s_pad = sem("s_pad")
        s_dst = sem("s_dst")
        s_src = sem("s_src")
        s_idx0 = sem("s_idx0")
        s_x = sem("s_x")
        s_iota = sem("s_iota")
        s_dve = sem("s_dve")
        s_ext = sem("s_ext")
        s_extp = sem("s_extp")
        s_setup = sem("s_setup")
        s_node = sem("s_node")
        s_tab = sem("s_tab")
        s_tabr = sem("s_tabr")
        s_str = sem("s_str")
        s_sts = sem("s_sts")
        s_nmi = sem("s_nmi")
        s_nmt = sem("s_nmt")
        s_nmc = sem("s_nmc")
        s_nmo = sem("s_nmo")
        s_accd = sem("s_accd")
        s_step = sem("s_step")
        s_th = sem("s_th")
        s_sqi = sem("s_sqi")
        s_sqo = sem("s_sqo")
        s_thi = sem("s_thi")
        s_row = sem("s_row")
        s_rowv = sem("s_rowv")
        s_vtab = sem("s_vtab")
        s_fin = sem("s_fin")
        s_out = sem("s_out")

        oh_ready = [[sem(f"oh_ready{p}_{h}") for h in range(2)] for p in range(4)]
        oh_used = [[sem(f"oh_used{p}_{h}") for h in range(2)] for p in range(4)]
        row_used = [sem(f"row_used{p}") for p in range(4)]
        ea_in = [sem(f"ea_in{b}") for b in range(2)]
        ea_cp = sem("ea_cp")
        ea_lo = sem("ea_lo")
        idx_in = [[sem(f"idx_in{p}_{b}") for b in range(2)] for p in range(5)]
        g_in = [[sem(f"g_in{p}_{b}") for b in range(2)] for p in range(5)]
        g_used = {p: sem(f"g_used{p}") for p in (3, 4)}
        vb_in = {p: [sem(f"vb_in{p}_{k}") for k in range(2)] for p in (2, 3, 4)}
        hh_done = {p: sem(f"hh_done{p}") for p in (2, 3, 4)}
        oht_done = {p: sem(f"oht_done{p}") for p in (2, 3, 4)}
        gm_done = {p: sem(f"gm_done{p}") for p in (2, 3, 4)}
        mk_done = {p: sem(f"mk_done{p}") for p in (2, 3, 4)}
        rd_done = sem("rd_done")
        mk_used = {p: sem(f"mk_used{p}") for p in (3, 4)}
        eat_in = [[sem(f"eat_in{l}_{b}") for b in range(2)] for l in range(2)]
        h_mm = [sem(f"h_mm{l}") for l in range(2)]
        h_act = [sem(f"h_act{l}") for l in range(2)]
        w_mm = [sem(f"w_mm{l}") for l in range(2)]
        p_done = [sem(f"p_done{l}") for l in range(2)]
        r_done = [sem(f"r_done{l}") for l in range(2)]
        q_done = [sem(f"q_done{l}") for l in range(2)]
        m_hi = [sem(f"m_hi{l}") for l in range(2)]
        m_lo = [sem(f"m_lo{l}") for l in range(2)]
        l_done = [sem(f"l_done{l}") for l in range(2)]
        a_abs = [sem(f"a_abs{l}") for l in range(2)]
        a_done = [sem(f"a_done{l}") for l in range(2)]
        o_done = [sem(f"o_done{l}") for l in range(2)]
        sc_mm = [sem(f"sc_mm{l}") for l in range(2)]
        vp_done = sem("vp_done")
        vh_done = sem("vh_done")
        vl_done = sem("vl_done")

        tabs = [nc.dram_tensor(f"table{p}", (NP_, w), F32, kind="Internal").ap()
                for p, w in enumerate([D, MF, D, 3 * D // 2, 3 * D // 2])]
        tabw = [D, MF, D, 3 * D // 2, 3 * D // 2]
        vtab = nc.dram_tensor("vtab", (NSUP, SUP), F16, kind="Internal").ap()
        tabk = tabb[:, :, :, :].rearrange("p (h c) k f -> p c k h f", c=NC)
        tabc = tabb[:, :, :, :].rearrange("p (h c) k f -> p c h (k f)", c=NC)
        tabbf = tabb[:, :, :, :].rearrange("p q k f -> p q (k f)").bitcast(F32)

        block = ctx.enter_context(nc.Block())

        e3 = a["edge_attr_3"].rearrange("(s p t) c -> p s (t c)", p=P, t=T)
        e2 = a["edge_attr_2"].rearrange("(s p t) c -> p s (t c)", p=P, t=T)
        e16 = a["edge_attr_16"].rearrange("(s p t) c -> s p (t c)", p=P, t=T)
        srcv = a["src"].rearrange("(s p t) -> p s t", p=P, t=T)
        dstv = a["dst"].rearrange("(s p t) -> p s t", p=P, t=T)
        gidx = [a["dst"], a["dst"], a["src"], a["src"], a["src"]]
        gidxv = [g.rearrange("(s p t) -> s p t", p=P, t=T) for g in gidx]

        def load_window(eng, s, table=None):
            word = eng.value_load((win if table is None else table)[0:1, bass.ds(s, 1)], min_val=0, max_val=(1 << 23) - 1)
            lo = eng.snap(word & 31, min_val=0, max_val=NB - 1)
            hi = eng.snap((word >> 5) & 31, min_val=1, max_val=NB)
            off = eng.snap(word >> 10, min_val=0, max_val=4096)
            return lo, hi, off

        @block.sync
        def _(sp):
            sp.dma_start(dst_i[:, :, :], dstv).then_inc(s_dst, 16)
            sp.dma_start(src_i[:, :, :], srcv).then_inc(s_src, 16)
            sp.dma_start(rhat[:, :, :, :].rearrange("p s t c -> p s (t c)"), e3).then_inc(s_idx0, 16)
            sp.dma_start(ea2[:, :, :, :].rearrange("p s t c -> p s (t c)"), e2).then_inc(s_idx0, 16)
            sp.dma_start(x[:, :, :], a["x"].rearrange("(q p) f -> p q f", p=P)).then_inc(s_x, 16)
            sp.wait_ge(s_pad, 1)
            sp.dma_start(row_i, a["src_row"]).then_inc(s_row, 16)
            for l in range(2):
                sp.dma_start(w1[l][0:EK, :], a[f"w1_{l}"]).then_inc(s_par, 16)
                sp.dma_start(b1[l][:, :], a[f"b1_{l}"].rearrange("(k o) -> k o", o=1)).then_inc(s_par, 16)
                sp.dma_start(w2[l][0:EK + 1, :], a[f"w2_{l}"]).then_inc(s_par, 16)
            sp.dma_start(wst[0:2 * D, :], a["w_enet"]).then_inc(s_par, 16)
            sp.dma_start(wst[2 * D:3 * D, :], a["b_enet"]).then_inc(s_par, 16)
            sp.dma_start(wst[3 * D:4 * D, :], a["w_root"]).then_inc(s_par, 16)
            sp.dma_start(gw1[:, :], a["gw1"]).then_inc(s_par, 16)
            sp.dma_start(gw2[:, :], a["gw2"]).then_inc(s_par, 16)
            for i, n in enumerate(["gs0", "bs0", "gv0", "gs1", "bs1", "bias", "gamma", "beta", "gb1"]):
                k = a[n].shape[0]
                sp.dma_start(par[:, i, 0:k], a[n].rearrange("(o k) -> o k", o=1).broadcast_to([P, k])).then_inc(s_par, 16)
            sp.dma_start(c2[:, :], a["gb2"].rearrange("(o k) -> o k", o=1).broadcast_to([P, D])).then_inc(s_par, 16)

            sp.wait_ge(s_rowv, 1)
            sp.dma_start(vtab, row_v).then_inc(s_vtab, 16)

            with sp.Fori(0, PAIRS) as i:
                for b in range(2):
                    sp.wait_ge(ea_lo, i * 2 + b + 1)
                    sp.dma_start(ea16[:, b, :, :].rearrange("p t f -> p (t f)"),
                                 e16[bass.ds(i * 2 + b, 1), :, :].rearrange("o p f -> p (o f)")).then_inc(ea_in[b], 16)

            def store_table(p):
                sp.wait_ge(s_tabr, p + 1)
                rows = tab[:, :, 0:tabw[p]] if p < 3 else tabbf
                sp.dma_start(tabs[p].rearrange("(q p) f -> p q f", p=P), rows).then_inc(s_tab, 16)

            def load_idx(p, b, s):
                sp.dma_start(idx[:, b, :], gidxv[p][bass.ds(s, 1), :, :].rearrange("o p t -> p (o t)")).then_inc(idx_in[p][b], 16)

            def load_eat(l, b, s, n=None):
                sp.wait_ge(h_mm[l], (s if n is None else n) * 2 + 1)
                sp.dma_start(eat[0:EK, b, :], a["eat"][bass.ds(s, 1), :, :].rearrange("o k n -> k (o n)")).then_inc(eat_in[l][b], 16)

            for p in range(2):
                store_table(p)
                for b in range(2):
                    load_eat(p, b, b)
                    load_idx(p, b, b)
                with sp.Fori(1, PAIRS) as i:
                    for b in range(2):
                        load_eat(p, b, i * 2 + b)
                        sp.wait_ge(g_in[p][b], i * 16 * T)
                        load_idx(p, b, i * 2 + b)
                load_eat(p, 0, NSUP - 1, NSUP)

            def load_vb(p, k, s):
                sp.dma_start(vb[:, k, :], vtab[bass.ds(s, 1), :].broadcast_to([P, SUP])).then_inc(vb_in[p][k], 16)

            def refill(p, i, k):
                sp.wait_ge(g_in[p][k], i * 16 * T)
                load_idx(p, k, i * 4 + 2 * k)
                sp.wait_ge(oht_done[p], (i * 2 + k - 1) * NC)
                load_vb(p, k, i * 4 + 2 * k + 1)

            for p in (2, 3, 4):
                store_table(p)
                for k in range(2):
                    load_vb(p, k, 2 * k + 1)
                    load_idx(p, k, 2 * k)
                with sp.Fori(1, QUADS) as i:
                    for k in range(2):
                        refill(p, i, k)
                refill(p, QUADS, 0)
            sp.wait_ge(s_fin, 1)
            full = N // P
            sp.dma_start(a["out"][0:full * P, :].rearrange("(q p) f -> p q f", p=P), x[:, 0:full, :]).then_inc(s_out, 16)
            sp.dma_start(a["out"][full * P:N, :], x[0:N - full * P, full, :]).then_inc(s_out, 16)
            sp.wait_ge(s_out, 32)
            sp.wait_ge(s_tab, 16 * 5)

        @block.gpsimd
        def _(pool):
            nc.gpsimd.iota(iota_i[:, :], [[1, NP_]], base=0, channel_multiplier=0).then_inc(s_iota, 1)
            nc.gpsimd.iota(pid_i[:, :], [[0, 1]], base=0, channel_multiplier=1).then_inc(s_iota, 1)
            pool.wait_ge(s_ext, 1)
            nc.gpsimd.partition_all_reduce(extp[:, :, :].rearrange("p a s -> p (a s)"),
                                           ext[:, :, :].rearrange("p a s -> p (a s)"), P, RMAX).then_inc(s_extp, 1)
            pool.sem_inc(ea_lo, 2)

            def split_low(s, b, n):
                pool.wait_ge(ea_cp, s + 1)
                nc.gpsimd.tensor_tensor(vals[:, n, :, D + 1:2 * D + 1], ea16[:, b, :, :],
                                        vals[:, n, :, 0:D].bitcast(F32), ALU.subtract).then_inc(ea_lo, 1)

            with pool.Fori(0, QUADS) as i:
                for n in range(4):
                    split_low(i * 4 + n, n % 2, n)
            for n in range(2):
                split_low(NSUP - 2 + n, n, n)

            def gather(p, b, seen):
                pool.sem_inc(s_step, 1)
                pool.wait_ge(idx_in[p][b], seen * 16)
                pool.sem_inc(s_step, 1)
                for t in range(T):
                    nc.gpsimd.indirect_dma_start(
                        out=gb[:, b, t, 0:tabw[p]], out_offset=None, in_=tabs[p],
                        in_offset=bass.IndirectOffsetOnAxis(ap=idx[:, b, t:t + 1], axis=0)).then_inc(g_in[p][b], 16)

            for p in range(2):
                pool.wait_ge(s_tab, 16 * (p + 1))
                with pool.Fori(0, PAIRS) as i:
                    for b in range(2):
                        s = i * 2 + b
                        pool.wait_ge(p_done[p], s * T + 1)
                        gather(p, b, i + 1)
            for p in (2, 3, 4):
                def gather_pair(i, k):
                    if p == 2:
                        pool.wait_ge(vp_done, (i * 2 + k) * 6 + 1)
                    else:
                        pool.wait_ge(g_used[p], i * 2 + k + 1)
                    gather(p, k, i + 1)

                pool.wait_ge(s_tab, 16 * (p + 1))
                with pool.Fori(0, QUADS) as i:
                    for k in range(2):
                        gather_pair(i, k)
                gather_pair(QUADS, 0)

        @block.scalar
        def _(act):
            taken = [0]

            def root(out, in_):
                act.wait_ge(s_sqi, taken[0] + 1)
                nc.scalar.activation(out, in_, ACT.Sqrt).then_inc(s_sqo, 1)
                taken[0] += 1

            def node_root():
                root(r1_root[:, :], r1[:, :])

            def stat_root():
                root(sv_root[:, :], sv[:, 0:D])

            root(rn_root, rn[:, :, :].rearrange("p s t -> p (s t)"))
            def split_high(s, b, n, seen):
                act.wait_ge(ea_in[b], seen * 16)
                act.wait_ge(row_used[0], s + 1)
                nc.scalar.activation(vals[:, n, :, 0:D], ea16[:, b, :, :], ACT.Copy).then_inc(ea_cp, 1)

            with act.Fori(0, QUADS) as i:
                for n in range(4):
                    split_high(i * 4 + n, n % 2, n, i * 2 + n // 2 + 1)
            for n in range(2):
                split_high(NSUP - 2 + n, n, n, PAIRS)
            act.wait_ge(s_par, 16 * 21)
            node_root()
            node_root()
            for l in range(2):
                act.sem_inc(a_done[l], 2)
                def hidden(s, b, c):
                    act.wait_ge(h_mm[l], s * 2 + c + 4)
                    if c == 0:
                        act.wait_ge(w_mm[l], s * T + 1)
                    nc.scalar.activation(ht[0:EK, b, c * 512:(c + 1) * 512], ps[0:EK, 5, :], ACT.Relu,
                                         bias=b1[l][:, 0:1]).then_inc(h_act[l], 1)

                def source_onehots(s, b, t0, t1):
                    act.wait_ge(sc_mm[l], s * T + t1 + 4)
                    for t in range(t0, t1):
                        nc.scalar.activation(oh5[:, b, t, :], iota_f[:, 0:CW], ACT.Abs,
                                             bias=src_n[:, bass.ds(s, 1), t]).then_inc(a_abs[l], 1)
                    act.wait_ge(a_abs[l], s * AT + t1)
                    nc.scalar.activation(oh5[:, b, t0:t1, :], oh5[:, b, t0:t1, :].bitcast(F32),
                                         ACT.Relu, bias=ones[:, 0:1], scale=-1.0).then_inc(a_done[l], 1)

                hidden(0, 0, 0)
                hidden(0, 0, 1)
                with act.Fori(0, PAIRS) as i:
                    for b in range(2):
                        s = i * 2 + b
                        source_onehots(s, b, 0, 4)
                        hidden(s + 1, 1 - b, 0)
                        source_onehots(s, b, 4, AT)
                        hidden(s + 1, 1 - b, 1)
                stat_root()
                if l == 0:
                    stat_root()
                else:
                    node_root()
            with act.Fori(0, PAIRS) as i:
                for b in range(2):
                    s = i * 2 + b
                    act.wait_ge(vp_done, s * 3 + 13)
                    act.wait_ge(row_used[1], s + 1)
                    nc.scalar.activation(v96[:, b, :, 0, :], v48[:, b, :, :], ACT.Copy).then_inc(vh_done, 1)
            stat_root()
            node_root()
            for k in range(2):
                act.wait_ge(s_thi, k + 1)
                nc.scalar.activation(hh[:, :, :], t1[:, :, 0:D], ACT.Tanh).then_inc(s_th, 1)
            node_root()

        @block.tensor
        def _(pe):
            def zero_bank(bk):
                return nc.tensor.matmul(ps[:, bk, :], zeros[:, 0:P], zeros[:, :], start=True, stop=False, skip_group_check=True)

            def pair_windows(w, j, rhs_of, out_of):
                lo, hi, off = load_window(pe, j, win2)
                with pe.Fori(lo, hi) as c:
                    c = nc.s_assert_within(c, 0, NB - 1, skip_runtime_bounds_check_because="a block index out of the window table")
                    out = out_of(c)
                    for h in range(2):
                        pe.wait_ge(oh_ready[w][h], off + c + 1)
                        for t in range(T):
                            mm = nc.tensor.matmul(out, oh_r[:, h, t, :], rhs_of(h, t),
                                                  start=False, stop=False, skip_group_check=True)
                        mm.then_inc(oh_used[w][h], 1)

            def partition_sum(k):
                pe.wait_ge(s_str, k + 1)
                nc.tensor.matmul(ps[:, 5, 0:32], ones[:, :], stat[:, :], start=True, stop=True,
                                 skip_group_check=True).then_inc(s_sts, 1)

            def node_product(k, rows, wts):
                K = wts.shape[0]
                pe.wait_ge(s_nmi, k + 1)

                def block_products(j):
                    pe.wait_ge(s_nmc, k * 7 + j + 1)
                    for q in range(4 * j, min(4 * j + 4, NB)):
                        mm = nc.tensor.matmul(ps[:, 5, 64 + q * D:64 + (q + 1) * D], xt[0:K, q, :], wts,
                                              start=True, stop=True, skip_group_check=True)
                    return mm

                for j in range(7):
                    for q in range(4 * j, min(4 * j + 4, NB)):
                        tr = nc.tensor.transpose(ps[0:K, TBANK[j], (q % 4) * P:(q % 4 + 1) * P], rows(q), ident[:, :])
                    tr.then_inc(s_nmt, 1)
                    if j > 0:
                        block_products(j - 1)
                block_products(6).then_inc(s_nmo, 1)

            pe.wait_ge(s_setup, 1)
            for w in range(4):
                for h in range(2):
                    pe.sem_inc(oh_used[w][h], BIAS + 1)
            pe.sem_inc(row_used[0], 4)
            pe.sem_inc(row_used[1], 2)
            pe.wait_ge(s_par, 16 * 21)

            for bk in range(4):
                zero_bank(bk)
            def mean_step(j, k):
                pe.wait_ge(ea_cp, j * 2 + 2)
                pe.wait_ge(ea_lo, j * 2 + 4)
                pair_windows(0, j, lambda b, t: vals[:, 2 * k + b, t, :], lambda c: psf[:, bass.ds(c * 64, 2 * (D + 1))])
                nc.tensor.matmul(ps[:, 6, 0:32], zeros[:, 0:P], zeros[:, 0:32], start=True, stop=True)\
                    .then_inc(row_used[0], 2)

            with pe.Fori(0, QUADS) as i:
                for k in range(2):
                    mean_step(i * 2 + k, k)
            mean_step(PAIRS - 1, 0)
            nc.tensor.matmul(ps[:, 6, 0:32], zeros[:, 0:P], zeros[:, 0:32], start=True, stop=True).then_inc(s_accd, 1)

            for l in range(2):
                W = NH * MP[l]
                pe.wait_ge(s_node, l + 1)
                pe.sem_inc(h_mm[l], 3)
                pe.sem_inc(w_mm[l], 9)
                pe.sem_inc(sc_mm[l], 9)
                for bk in range(5):
                    zero_bank(bk)

                def scatter_tile(s, b, t):
                    if t < LAG:
                        if t == 1:
                            pe.wait_ge(o_done[l], s * 4 + 1)
                        b, t = b, t + T - LAG
                    else:
                        b, t = 1 - b, t - LAG
                        if t % 2 == 0:
                            pe.wait_ge(o_done[l], s * 4 + t // 2 + 2)
                        if t % 4 == 0:
                            pe.wait_ge(a_done[l], s * 2 + t // 4 + 1)
                    for c in range(NC):
                        out = ps[:, c, 0:W] if l == 0 else ps[:, c // 3, (c % 3) * W:(c % 3 + 1) * W]
                        mm = nc.tensor.matmul(out, oh5[:, b, t, c * P:(c + 1) * P], big[:, b, t, 0:W],
                                              start=False, stop=False, skip_group_check=True)
                    mm.then_inc(sc_mm[l], 1)

                def hidden(s, b, n, c):
                    if c == 0:
                        pe.wait_ge(eat_in[l][b], n * 16)
                    pe.wait_ge(h_act[l], s * 2 + c + 1)
                    nc.tensor.matmul(ps[:, 5, :], w1[l][:, :], eat[:, b, c * 512:(c + 1) * 512],
                                     start=True, stop=True).then_inc(h_mm[l], 1)

                hidden(0, 0, 1, 0)
                hidden(0, 0, 1, 1)
                with pe.Fori(0, PAIRS) as i:
                    for b in range(2):
                        s = i * 2 + b
                        for t in range(T):
                            if t % 4 == 0:
                                pe.wait_ge(h_act[l], s * 2 + t // 4 + 2)
                            pe.wait_ge(p_done[l], s * T + t + 10 - len(WBANKS[l]))
                            nc.tensor.matmul(ps[:, WBANKS[l][t % len(WBANKS[l])], 0:MJ * D], ht[:, b, t * P:(t + 1) * P],
                                             w2[l][:, :], start=True, stop=True).then_inc(w_mm[l], 1)
                            scatter_tile(s, b, t)
                            if t in (3, 5):
                                hidden(s + 1, 1 - b, i + 1 + b, t // 2 - 1)
                for t in range(T):
                    scatter_tile(NSUP, 0, t)
                for t in range(LAG):
                    scatter_tile(NSUP + 1, 1, t)
                pe.wait_ge(h_act[l], (NSUP + 1) * 2 + 1)
                nc.tensor.matmul(ps[:, 7, 0:32], zeros[:, 0:P], zeros[:, 0:32], start=True, stop=True).then_inc(s_accd, 1)
                if l == 0:
                    for k in range(3):
                        partition_sum(k)
                else:
                    for k in range(3, 5):
                        partition_sum(k)

            pe.wait_ge(s_node, 3)
            pe.sem_inc(gm_done[2], 3)
            for bk in range(5):
                zero_bank(bk)

            def gather_rows(j, k, g):
                if g == 0:
                    pe.wait_ge(oht_done[2], j * NC + NC)
                pe.wait_ge(mk_done[2], j * 2 + g + 2)
                for u in range(4):
                    e = (4 * g + u) * P
                    for c in range(NC):
                        for part in range(3):
                            mm = nc.tensor.matmul(ps[:, 5 + g, u * AW:(u + 1) * AW], oht[:, k, c, e:e + P],
                                                  tabk[:, c, part, :, :], start=(c + part == 0),
                                                  stop=(c == NC - 1 and part == 2), skip_group_check=True)
                mm.then_inc(gm_done[2], 1)

            def edge_step(j, i, k, ahead):
                if ahead:
                    gather_rows(j + 1, 1 - k, 0)
                    gather_rows(j + 1, 1 - k, 1)
                pe.wait_ge(vl_done, j * 2 + 4)
                pair_windows(1, j, lambda b, t: v96[:, b, t, :, :].rearrange("p k f -> p (k f)"),
                             lambda c: psf[:, bass.ds(pe.snap(c * EW + ((c * 52) >> 8) * (512 - EBANK * EW),
                                                              min_val=0, max_val=5 * 512 - EW), EW)])
                nc.tensor.matmul(ps[:, 7, 0:32], zeros[:, 0:P], zeros[:, 0:32], start=True, stop=True)\
                    .then_inc(row_used[1], 2)

            gather_rows(0, 0, 0)
            gather_rows(0, 0, 1)
            with pe.Fori(0, QUADS) as i:
                for k in range(2):
                    edge_step(i * 2 + k, i, k, True)
            edge_step(PAIRS - 1, QUADS, 0, False)
            nc.tensor.matmul(ps[:, 7, 0:32], zeros[:, 0:P], zeros[:, 0:32], start=True, stop=True).then_inc(s_accd, 1)
            node_product(0, lambda q: acc[:, q, :], wst[:, :])
            for k in range(5, 7):
                partition_sum(k)
            node_product(1, lambda q: x[:, q, :], gw1[:, :])

            for p in (3, 4):
                w = p - 1
                pe.wait_ge(s_node, p + 1)
                pe.sem_inc(gm_done[p], 5)
                pe.sem_inc(mk_used[p], 2)
                for bk in range(5):
                    zero_bank(bk)

                def sums_of(c):
                    at = pe.snap(c * AW + ((c * 43) >> 8) * (512 - ABANK * AW), min_val=0, max_val=5 * 512 - AW)
                    return at

                def gather_tiles(j, k, g):
                    if g == 0:
                        pe.wait_ge(oht_done[p], j * NC + NC)
                        pe.wait_ge(mk_done[p], j * 4 + 5)
                    if g == 3:
                        pe.wait_ge(mk_done[p], j * 4 + 6)
                    for u in range(2):
                        e = (2 * g + u) * P
                        for c in range(NC):
                            mm = nc.tensor.matmul(ps[:, 5 + g % 3, u * GW:(u + 1) * GW], oht[:, k, c, e:e + P],
                                                  tabc[:, c, :, :], start=(c == 0), stop=(c == NC - 1),
                                                  skip_group_check=True)
                    mm.then_inc(gm_done[p], 1)

                def idle_matmul():
                    return nc.tensor.matmul(ps[:, 4, 480:512], zeros[:, 0:P], zeros[:, 0:32], start=False, stop=False,
                                            skip_group_check=True)

                def step(j, i, k, ahead):
                    s = i * 4 + 2 * k
                    gather_tiles(j, k, 3)
                    if ahead:
                        gather_tiles(j + 1, 1 - k, 0)
                    pe.wait_ge(g_in[p][k], (i + 1) * 16 * T)
                    conv_windows(w, s, lambda t: [gb[:, k, t, 0:3 * D // 2].bitcast(BF16)], 3 * D)
                    idle_matmul().then_inc(g_used[p], 1)
                    if ahead:
                        gather_tiles(j + 1, 1 - k, 1)
                    pe.wait_ge(mk_done[p], j * 4 + 9)
                    conv_windows(w, s + 1, lambda t: [mk[:, k, t, n * AW:(n + 1) * AW] for n in range(3)], AW)
                    idle_matmul().then_inc(mk_used[p], 1)
                    if ahead:
                        gather_tiles(j + 1, 1 - k, 2)

                def conv_windows(w, s, parts_of, width):
                    lo, hi, off = load_window(pe, s)
                    with pe.Fori(lo, hi) as c:
                        c = nc.s_assert_within(c, 0, NB - 1, skip_runtime_bounds_check_because="a block index out of the window table")
                        at = sums_of(c)
                        for h in range(2):
                            pe.wait_ge(oh_ready[w][h], off + c + 1)
                            for u in range(T // 2):
                                for part in parts_of(h * (T // 2) + u):
                                    mm = nc.tensor.matmul(psf[:, bass.ds(at, width)], oh_b[:, h, u, :], part,
                                                          start=False, stop=False, skip_group_check=True)
                            mm.then_inc(oh_used[w][h], 1)

                for g in range(3):
                    gather_tiles(0, 0, g)
                with pe.Fori(0, QUADS) as i:
                    for k in range(2):
                        step(i * 2 + k, i, k, True)
                step(PAIRS - 1, QUADS, 0, False)
                idle_matmul().then_inc(s_accd, 1)
                if p == 3:
                    node_product(2, lambda q: hh[:, q, :], gw2[:, :])

        @block.vector
        def _(dve):
            V = nc.vector
            chain = [0]

            def link(ins):
                chain[0] += 1
                ins.then_inc(s_dve, 1)
                dve.wait_ge(s_dve, chain[0])

            def bc(ap, n):
                return repeat(ap, len(ap.shape), n)

            roots = [2]

            def square_root(v, root, tmp, k):
                dve.wait_ge(s_sqo, k)
                link(V.tensor_scalar(tmp, root, 1e-30, None, ALU.max))
                link(V.reciprocal(tmp, tmp))
                link(V.tensor_tensor(tmp, tmp, v, ALU.mult))
                link(V.tensor_tensor(root, root, tmp, ALU.add))
                link(V.tensor_scalar(root, root, 0.5, None, ALU.mult))

            link(V.memset(zeros[:, :], 0.0))
            link(V.memset(ones[:, :], 1.0))
            link(V.memset(vals[:, :, :, D:D + 1].bitcast(F32), 1.0))
            link(V.memset(vals[:, :, :, 2 * D + 1:2 * D + 2].bitcast(F32), 0.0))
            link(V.memset(parts[0][:, :, :, MF:MF + 1].bitcast(F32), 1.0))
            link(V.memset(parts[0][:, :, :, 2 * MF + 1:2 * MF + 2].bitcast(F32), 0.0))
            link(V.memset(eat[:, :, :], 0.0))
            for l in range(2):
                link(V.memset(w1[l][:, :], 0.0))
                link(V.memset(w2[l][:, :], 0.0))
            dve.sem_inc(s_pad, 1)
            link(V.memset(stat[:, :], 0.0))
            dve.wait_ge(s_iota, 2)
            link(V.tensor_copy(iota_f[:, :], iota_i[:, :]))
            link(V.tensor_copy(pid_f[:, :], pid_i[:, :]))
            link(V.tensor_scalar(ident[:, :], iota_f[:, 0:P], pid_f[:, 0:1], None, ALU.is_equal))
            link(V.tensor_scalar(node_id[:, :], iota_f[:, 0:NB], float(P), pid_f[:, 0:1], ALU.mult, ALU.add))
            link(V.tensor_scalar(mask[:, :], node_id[:, :], float(N), None, ALU.is_lt))
            dve.wait_ge(s_dst, 16)
            link(V.tensor_copy(dst_f[:, :, :], dst_i[:, :, :]))
            link(V.tensor_scalar(neg_dst[:, :, :], dst_f[:, :, :], -1.0, None, ALU.mult))
            link(V.tensor_reduce(ext[:, 0, :], dst_f[:, :, :], AX.X, ALU.max))
            V.tensor_reduce(ext[:, 1, :], neg_dst[:, :, :], AX.X, ALU.max).then_inc(s_ext, 1)
            dve.wait_ge(s_extp, 1)
            link(V.tensor_copy(ext_i[:, 0, :], extp[:, 0, :]))
            link(V.tensor_scalar(ext_i[:, 1, :], extp[:, 1, :], -1.0, None, ALU.mult))
            link(V.tensor_scalar(blk_i[:, :, :], ext_i[:, :, :], 7, None, ALU.logical_shift_right))
            link(V.tensor_copy(blk[:, :, :], blk_i[:, :, :]))
            link(V.tensor_reduce(blk2[:, 0, :], blk[:, 0, :].rearrange("p (j b) -> p j b", b=2), AX.X, ALU.max))
            link(V.tensor_reduce(blk2[:, 1, :], blk[:, 1, :].rearrange("p (j b) -> p j b", b=2), AX.X, ALU.min))
            for bl, table, n in ((blk, win, NSUP), (blk2, win2, PAIRS)):
                cn, cu, wf = cnt_w[:, 0:n], cum_w[:, 0:n], win_f[:, 0:n]
                link(V.tensor_tensor(cn, bl[:, 0, :], bl[:, 1, :], ALU.subtract))
                link(V.tensor_scalar(cn, cn, 1.0, None, ALU.add))
                link(V.tensor_tensor_scan(cu, ones[:, 0:n], cn, 0.0, ALU.mult, ALU.add))
                link(V.tensor_tensor(cu, cu, cn, ALU.subtract))
                link(V.tensor_tensor(cu, cu, bl[:, 1, :], ALU.subtract))
                link(V.tensor_scalar(wf, bl[:, 0, :], 32.0, 32.0 + 1024.0 * BIAS, ALU.mult, ALU.add))
                link(V.tensor_tensor(wf, wf, bl[:, 1, :], ALU.add))
                link(V.tensor_scalar(cu, cu, 1024.0, None, ALU.mult))
                link(V.tensor_tensor(wf, wf, cu, ALU.add))
                link(V.tensor_copy(table[:, :], wf))
            for w in range(4):
                for h in range(2):
                    dve.sem_inc(oh_ready[w][h], BIAS)
            link(V.memset(sv[:, :], 1.0))
            V.memset(sm[:, :], 0.0).then_inc(s_setup, 1)

            dve.wait_ge(s_src, 16)
            link(V.tensor_copy(src_f[:, :, :], src_i[:, :, :]))
            link(V.tensor_scalar(src_h[:, :, :], src_f[:, :, :], float(CW), None, ALU.is_ge))
            for k in range(2, NH):
                link(V.scalar_tensor_tensor(out=src_h[:, :, :], in0=src_f[:, :, :], scalar=float(k * CW),
                                            in1=src_h[:, :, :], op0=ALU.is_ge, op1=ALU.add))
            link(V.scalar_tensor_tensor(out=src_v[:, :, :], in0=src_h[:, :, :], scalar=-float(CW),
                                        in1=src_f[:, :, :], op0=ALU.mult, op1=ALU.add))
            link(V.tensor_scalar(src_n[:, :, :], src_v[:, :, :], -1.0, None, ALU.mult))
            dve.wait_ge(s_row, 16)
            link(V.tensor_copy(row_f, row_i))
            link(V.tensor_scalar(row_h, row_f, float(CW), None, ALU.is_ge))
            for k in range(2, NH):
                link(V.scalar_tensor_tensor(out=row_h, in0=row_f, scalar=float(k * CW), in1=row_h,
                                            op0=ALU.is_ge, op1=ALU.add))
            V.scalar_tensor_tensor(out=row_v, in0=row_h, scalar=-float(CW), in1=row_f,
                                   op0=ALU.mult, op1=ALU.add).then_inc(s_rowv, 1)
            dve.wait_ge(s_rowv, 1)
            link(V.memset(ht[:, :, :], 1.0))
            link(V.tensor_scalar(pid_c[:, :], iota_f[:, 0:NC], float(P), pid_f[:, 0:1], ALU.mult, ALU.add))

            dve.wait_ge(s_idx0, 32)
            rv = rhat[:, :, :, :].rearrange("p s t c -> p (s t) c")
            rnf = rn[:, :, :].rearrange("p s t -> p (s t)")
            rq = rsq.rearrange("p (n c) -> p n c", c=3)
            link(V.tensor_tensor(rq, rv, rv, ALU.mult))
            V.tensor_reduce(rnf, rq, AX.X, ALU.add).then_inc(s_sqi, 1)
            square_root(rnf, rn_root, rn_t, 1)
            link(V.tensor_scalar(rnf, rn_root, 1e-12, None, ALU.add))
            link(V.reciprocal(rnf, rnf))
            link(V.tensor_tensor(rv, rv, bc(rnf, 3), ALU.mult))

            def window_onehots(w, s):
                lo, hi, off = load_window(dve, s)
                with dve.Fori(lo, hi) as c:
                    c = nc.s_assert_within(c, 0, NB - 1, skip_runtime_bounds_check_because="a block index out of the window table")
                    for h in range(2):
                        dve.wait_ge(oh_used[w][h], off + c + 1)
                        d = dst_f[:, bass.ds(s, 1), h * 4:h * 4 + 4].rearrange("p o t -> p (o t)")
                        cols = repeat(iota_f[:, bass.ds(c * P, P)], 1, T // 2)
                        V.tensor_tensor(oh_b[:, h, :, :], bc(d, P), cols, ALU.is_equal).then_inc(oh_ready[w][h], 1)

            def one_sup(ap3, s):
                return ap3[:, bass.ds(s, 1), :].rearrange("p o t -> p (o t)")

            def pair_onehots(w, j):
                lo, hi, off = load_window(dve, j, win2)
                with dve.Fori(lo, hi) as c:
                    c = nc.s_assert_within(c, 0, NB - 1, skip_runtime_bounds_check_because="a block index out of the window table")
                    for h in range(2):
                        dve.wait_ge(oh_used[w][h], off + c + 1)
                        cols = repeat(iota_f[:, bass.ds(c * P, P)], 1, T)
                        V.tensor_tensor(oh_r[:, h, :, :], bc(one_sup(dst_f, j * 2 + h), P), cols,
                                        ALU.is_equal).then_inc(oh_ready[w][h], 1)

            with dve.Fori(0, PAIRS) as i:
                pair_onehots(0, i)

            def layer_norm(xx):
                link(V.tensor_reduce(r1[:, :], xx, AX.X, ALU.add))
                link(V.tensor_scalar(r1[:, :], r1[:, :], 1.0 / D, None, ALU.mult))
                link(V.tensor_tensor(xx, xx, bc(r1[:, :], D), ALU.subtract))
                link(V.tensor_tensor(t2[:, :, 0:D], xx, xx, ALU.mult))
                link(V.tensor_reduce(r1[:, :], t2[:, :, 0:D], AX.X, ALU.add))
                roots[0] += 1
                V.tensor_scalar(r1[:, :], r1[:, :], 1.0 / D, EPS, ALU.mult, ALU.add).then_inc(s_sqi, 1)
                square_root(r1[:, :], r1_root[:, :], r1_t[:, :], roots[0])
                link(V.reciprocal(r1[:, :], r1_root[:, :]))
                link(V.tensor_tensor(xx, xx, bc(r1[:, :], D), ALU.mult))

            def table_parts(rows):
                link(V.tensor_copy(tabb[:, :, 0, :], rows))
                link(V.tensor_tensor(t2[:, :, 0:D], rows, tabb[:, :, 0, :], ALU.subtract))
                link(V.tensor_copy(tabb[:, :, 1, :], t2[:, :, 0:D]))
                link(V.tensor_tensor(t2[:, :, 0:D], t2[:, :, 0:D], tabb[:, :, 1, :], ALU.subtract))
                link(V.tensor_copy(tabb[:, :, 2, :], t2[:, :, 0:D]))

            def clear_scatter():
                link(V.memset(big[:, 0, T - LAG:T, :].bitcast(F32), 0.0))
                link(V.memset(oh5[:, 0, T - LAG:T, :].bitcast(F32), 0.0))
                link(V.memset(oh5[:, 1, :, :].bitcast(F32), 0.0))
                link(V.memset(oh_h[:, 1, :, :], 0.0))
                link(V.memset(msg[:, 1, :, :], 0.0))

            stats = [0]

            def node_sum(src, n):
                V.tensor_reduce(stat[:, 0:n], src.rearrange("p q f -> p f q"), AX.X, ALU.add).then_inc(s_str, 1)
                stats[0] += 1
                dve.wait_ge(s_sts, stats[0])

            def over_nodes(ap, f):
                return repeat(ap, 1, NB)

            def batch_norm(xx, g, b_):
                node_sum(xx, D)
                link(V.tensor_scalar(sm[:, 0:D], ps[:, 5, 0:D], 1.0 / N, None, ALU.mult))
                link(V.tensor_tensor(xx, xx, over_nodes(sm[:, 0:D], D), ALU.subtract))
                link(V.tensor_tensor(xx, xx, bc(mask[:, :], D), ALU.mult))
                link(V.tensor_tensor(t2[:, :, 0:D], xx, xx, ALU.mult))
                node_sum(t2[:, :, 0:D], D)
                roots[0] += 1
                V.tensor_scalar(sv[:, 0:D], ps[:, 5, 0:D], 1.0 / N, EPS, ALU.mult, ALU.add).then_inc(s_sqi, 1)
                square_root(sv[:, 0:D], sv_root[:, :], sv_t[:, :], roots[0])
                link(V.reciprocal(sv[:, 0:D], sv_root[:, :]))
                link(V.tensor_tensor(sv[:, 0:D], sv[:, 0:D], par[:, g, :], ALU.mult))
                link(V.tensor_tensor(xx, xx, over_nodes(sv[:, 0:D], D), ALU.mult))
                link(V.tensor_tensor(xx, xx, over_nodes(par[:, b_, :], D), ALU.add))

            dve.wait_ge(s_accd, 1)
            dve.wait_ge(s_x, 16)
            dve.wait_ge(s_par, 16 * 21)
            a0 = psf[:, 0:NB * 64].rearrange("p (q f) -> p q f", f=64)
            V.tensor_scalar(r1[:, :], a0[:, :, D], 1.0, None, ALU.add).then_inc(s_sqi, 1)
            square_root(r1[:, :], r1_root[:, :], r1_t[:, :], 2)
            link(V.reciprocal(dinv[:, :], r1_root[:, :]))
            link(V.tensor_scalar(rcd[:, :], a0[:, :, D], 1.0, None, ALU.max))
            link(V.reciprocal(rcd[:, :], rcd[:, :]))
            link(V.tensor_copy(t1[:, :, 0:D], a0[:, :, 0:D]))
            link(V.tensor_tensor(t1[:, :, 0:D], t1[:, :, 0:D], a0[:, :, D + 1:2 * D + 1], ALU.add))
            link(V.tensor_tensor(t1[:, :, 0:D], t1[:, :, 0:D], bc(rcd[:, :], D), ALU.mult))
            link(V.tensor_tensor(x[:, :, :], x[:, :, :], t1[:, :, 0:D], ALU.add))
            layer_norm(x[:, :, :])
            V.tensor_copy(tab[:, :, 0:D], x[:, :, :]).then_inc(s_tabr, 1)
            clear_scatter()
            dve.sem_inc(s_node, 1)

            for l in range(2):
                p = l
                dve.sem_inc(h_act[l], 1)
                dve.sem_inc(p_done[l], 9)
                dve.sem_inc(r_done[l], 2)
                dve.sem_inc(o_done[l], 1)
                dve.sem_inc(m_lo[l], 1)
                dve.sem_inc(l_done[l], 1)
                if l == 0:
                    dve.sem_inc(q_done[l], 1)
                W = MF if l == 0 else D
                L = W + 1 if l == 0 else W
                J_ = MJ if l == 0 else D
                m0 = NV if l == 0 else 0

                def split_messages(s, b):
                    dve.wait_ge(r_done[l], s * 4 + 2)
                    if l == 0:
                        dve.wait_ge(q_done[l], s + 1)
                    dve.wait_ge(o_done[l], s * 4 + 1)
                    V.tensor_copy(parts[l][:, b, :, 0:W], msg[:, b, :, m0:m0 + W]).then_inc(m_hi[l], 1)

                def low_messages(s, b):
                    dve.wait_ge(m_hi[l], s + 1)
                    V.tensor_tensor(parts[l][:, b, :, L:L + W], msg[:, b, :, m0:m0 + W],
                                    parts[l][:, b, :, 0:W].bitcast(F32), ALU.subtract).then_inc(m_lo[l], 1)

                def spread_messages(s, b, g):
                    if g == 0:
                        dve.wait_ge(l_done[l], s * 2 + 1)
                        dve.wait_ge(m_lo[l], s + 2)
                        dve.wait_ge(sc_mm[l], s * T + 1)
                    if g > 1:
                        dve.wait_ge(sc_mm[l], s * T + 2 * g - 2)
                    V.tensor_tensor(big[:, b, 2 * g:2 * g + 2, 0:NH * MP[l]].rearrange("p t (h f) -> p t h f", h=NH),
                                    repeat(parts[l][:, b, 2 * g:2 * g + 2, :].bitcast(F32), 2, NH),
                                    bc(oh_h[:, b, 2 * g:2 * g + 2, :], MP[l]), ALU.mult).then_inc(o_done[l], 1)

                with dve.Fori(0, PAIRS) as i:
                    for b in range(2):
                        s = i * 2 + b
                        rh = rhat[:, bass.ds(s, 1), :, :].rearrange("p o t c -> p (o t) c")
                        dve.wait_ge(g_in[p][b], (i + 1) * 16 * T)
                        if l == 1:
                            V.tensor_tensor(vprod[:, :, :, :], gb[:, b, :, 0:12].rearrange("p t (j c) -> p t j c", c=3),
                                            repeat(rh, 2, NV), ALU.mult).then_inc(q_done[l], 1)
                            dve.wait_ge(q_done[l], s * 2 + 1)
                            V.tensor_reduce(gb[:, b, :, 28:32], vprod[:, :, :, :], AX.X, ALU.add).then_inc(q_done[l], 1)
                            dve.wait_ge(q_done[l], s * 2 + 2)

                        def reduce_pair(g):
                            pv = prod[:, (2 * g) % 4:(2 * g) % 4 + 2, :].rearrange("p t (i j) -> p t i j", j=J_)
                            dve.wait_ge(p_done[l], s * T + 2 * g + 11)
                            if g == 0:
                                dve.wait_ge(m_lo[l], s + 1)
                            V.tensor_reduce(msg[:, b, 2 * g:2 * g + 2, 0:J_], pv.rearrange("p t i j -> p t j i"),
                                            AX.X, ALU.add).then_inc(r_done[l], 1)

                        for t in range(T):
                            dve.wait_ge(w_mm[l], s * T + t + 10)
                            if t % 2 == 0:
                                dve.wait_ge(r_done[l], s * 4 + t // 2 + 1)
                            xin = gb[:, b, t, 0:D] if l == 0 else gb[:, b, t, 12:32]
                            wv = ps[:, WBANKS[l][t % len(WBANKS[l])], 0:MJ * D].rearrange("p (i j) -> p i j", j=J_)
                            pv = prod[:, t % 4, :].rearrange("p (i j) -> p i j", j=J_)
                            V.tensor_tensor(pv, wv, bc(xin, J_), ALU.mult).then_inc(p_done[l], 1)
                            if t % 2 == 0 and t > 0:
                                reduce_pair(t // 2 - 1)
                            if t == 0:
                                split_messages(s, 1 - b)
                            if t == 1:
                                low_messages(s, 1 - b)
                            if t == 2:
                                dve.wait_ge(o_done[l], s * 4 + 1)
                                V.tensor_tensor(oh_h[:, b, :, :], bc(one_sup(src_h, s), NH), repeat(iota_f[:, 0:NH], 1, T),
                                                ALU.is_equal).then_inc(l_done[l], 1)
                            if t == 4:
                                dve.wait_ge(sc_mm[l], s * T + 12)
                                V.tensor_scalar(oh5[:, b, AT, :], iota_f[:, 0:CW], src_v[:, bass.ds(s, 1), AT], None,
                                                ALU.is_equal).then_inc(l_done[l], 1)
                            if t % 2 == 1:
                                spread_messages(s, 1 - b, t // 2)
                        reduce_pair(3)
                        if l == 0:
                            dve.wait_ge(r_done[l], s * 4 + 6)
                            V.tensor_tensor(msg[:, b, :, MJ:MJ + 12].rearrange("p t (j c) -> p t j c", c=3),
                                            bc(msg[:, b, :, 0:NV], 3), repeat(rh, 2, NV),
                                            ALU.mult).then_inc(q_done[l], 1)
                split_messages(NSUP, 1)
                low_messages(NSUP, 1)
                for g in range(4):
                    spread_messages(NSUP, 1, g)
                dve.wait_ge(s_accd, l + 2)
                if l == 0:
                    t1c = t1[:, :, :].rearrange("p (h c) f -> p h c f", c=NC)
                    rcc = rcs[:, :].rearrange("p (h c) -> p h c", c=NC)
                    for c in range(NC):
                        av = ps[:, c, 0:NH * MP[0]].rearrange("p (h f) -> p h f", h=NH)
                        link(V.tensor_scalar(rcc[:, :, c], av[:, :, MF], 1.0, None, ALU.max))
                        link(V.tensor_copy(t1c[:, :, c, 0:MF], av[:, :, 0:MF]))
                        link(V.tensor_tensor(t1c[:, :, c, 0:MF], t1c[:, :, c, 0:MF], av[:, :, MF + 1:2 * MF + 1], ALU.add))
                    link(V.reciprocal(rcs[:, :], rcs[:, :]))
                    link(V.tensor_tensor(rcs[:, :], rcs[:, :], mask[:, :], ALU.mult))
                    link(V.tensor_tensor(t1[:, :, 0:MF], t1[:, :, 0:MF], bc(rcs[:, :], MF), ALU.mult))
                    link(V.tensor_scalar(tab[:, :, 12:MF], t1[:, :, 0:D], 0.25, None, ALU.mult))
                    link(V.tensor_scalar(tab[:, :, 0:12], t1[:, :, D:MF], 0.25 * 3.0 ** 0.5, None, ALU.mult))
                    batch_norm(tab[:, :, 12:MF], GS0, BS0)
                    link(V.tensor_tensor(t2[:, :, 0:12], tab[:, :, 0:12], tab[:, :, 0:12], ALU.mult))
                    node_sum(t2[:, :, 0:12], 12)
                    link(V.tensor_copy(sm[:, 0:12], ps[:, 5, 0:12]))
                    link(V.tensor_reduce(sv[:, 0:NV], sm[:, 0:12].rearrange("p (j c) -> p j c", c=3), AX.X, ALU.add))
                    roots[0] += 1
                    V.tensor_scalar(sv[:, 0:D], sv[:, 0:D], 1.0 / (3 * N), EPS, ALU.mult, ALU.add).then_inc(s_sqi, 1)
                    square_root(sv[:, 0:D], sv_root[:, :], sv_t[:, :], roots[0])
                    link(V.reciprocal(sv[:, 0:D], sv_root[:, :]))
                    link(V.tensor_tensor(sv[:, 0:NV], sv[:, 0:NV], par[:, GV0, 0:NV], ALU.mult))
                    link(V.tensor_copy(sm[:, 0:12].rearrange("p (j c) -> p j c", c=3), bc(sv[:, 0:NV], 3)))
                    V.tensor_tensor(tab[:, :, 0:12], tab[:, :, 0:12], over_nodes(sm[:, 0:12], 12), ALU.mult).then_inc(s_tabr, 1)
                    clear_scatter()
                    dve.sem_inc(s_node, 1)
                else:
                    t1c = t1[:, :, :].rearrange("p (h c) f -> p h c f", c=NC)
                    for c in range(NC):
                        W5 = NH * MP[1]
                        av = ps[:, c // 3, (c % 3) * W5:(c % 3 + 1) * W5].rearrange("p (h f) -> p h f", h=NH)
                        link(V.tensor_copy(t1c[:, :, c, 0:D], av[:, :, 0:D]))
                        link(V.tensor_tensor(t1c[:, :, c, 0:D], t1c[:, :, c, 0:D], av[:, :, D:2 * D], ALU.add))
                    link(V.tensor_tensor(t1[:, :, 0:D], t1[:, :, 0:D], bc(rcs[:, :], D), ALU.mult))
                    link(V.tensor_scalar(t1[:, :, 0:D], t1[:, :, 0:D], float(MJ) ** -0.5, None, ALU.mult))
                    batch_norm(t1[:, :, 0:D], GS1, BS1)
                    link(V.tensor_tensor(x[:, :, :], x[:, :, :], t1[:, :, 0:D], ALU.add))
                    layer_norm(x[:, :, :])
                    dve.wait_ge(s_tab, 32)
                    V.tensor_copy(tab[:, :, 0:D], x[:, :, :]).then_inc(s_tabr, 1)
                    table_parts(x[:, :, :])
                    dve.sem_inc(s_node, 1)

            products = [0]

            def node_product(K):
                k = products[0]
                products[0] += 1
                for j in range(7):
                    dve.wait_ge(s_nmt, k * 7 + j + 1)
                    n = min(4, NB - 4 * j)
                    V.tensor_copy(xt[0:K, 4 * j:4 * j + n, :],
                                  ps[0:K, TBANK[j], 0:n * P].rearrange("k (n c) -> k n c", c=P)).then_inc(s_nmc, 1)
                dve.wait_ge(s_nmo, k + 1)
                return ps[:, 5, 64:64 + NB * D].rearrange("p (q f) -> p q f", f=D)

            def scaled_table(res):
                link(V.tensor_tensor(tab[:, :, 0:D], res, bc(dinv[:, :], D), ALU.mult))
                table_parts(tab[:, :, 0:D])
                dve.sem_inc(s_tabr, 1)

            def source_onehots(p, j, i, k, groups, cs):
                s = i * 4 + 2 * k + 1
                if 0 in cs:
                    dve.wait_ge(mk_done[p], j * groups + 1)
                    V.tensor_tensor(oh_h[:, k, :, :], bc(one_sup(src_h, s), NH), repeat(iota_f[:, 0:NH], 1, T),
                                    ALU.is_equal).then_inc(hh_done[p], 1)
                    dve.wait_ge(gm_done[p], j * groups + 1)
                    dve.wait_ge(vb_in[p][k], (i + 1) * 16)
                for c in cs:
                    V.tensor_scalar(oht[:, k, c, :], vb[:, k, :], pid_c[:, c:c + 1], None,
                                    ALU.is_equal).then_inc(oht_done[p], 1)

            def edge_network():
                dve.sem_inc(vp_done, 10)
                dve.sem_inc(vl_done, 2)
                dve.sem_inc(mk_done[2], 3)
                dve.sem_inc(rd_done, 3)

                def edge_products(s, b, rows):
                    dve.wait_ge(vl_done, s + 1)
                    for k in range(2):
                        ek = ea2[:, bass.ds(s, 1), :, k].rearrange("p o t -> p (o t)")
                        V.tensor_tensor(v48[:, b, :, k * D:(k + 1) * D], rows, bc(ek, D), ALU.mult).then_inc(vp_done, 1)
                    V.tensor_copy(v48[:, b, :, 2 * D:3 * D], rows).then_inc(vp_done, 1)

                def low_parts(s, b):
                    dve.wait_ge(vp_done, s * 3 + 13)
                    dve.wait_ge(vh_done, s + 1)
                    V.tensor_tensor(v96[:, b, :, 1, :], v48[:, b, :, :], v96[:, b, :, 0, :].bitcast(F32),
                                    ALU.subtract).then_inc(vl_done, 1)

                def select_rows(j, k, g):
                    dve.wait_ge(gm_done[2], j * 2 + g + 4)
                    if g == 0:
                        dve.wait_ge(rd_done, j * 2 + 1)
                        dve.wait_ge(hh_done[2], j + 1)
                    V.tensor_tensor(mkf[:, k, 4 * g:4 * g + 4, :].rearrange("p t (h f) -> p t h f", h=NH),
                                    ps[:, 5 + g, 0:4 * AW].rearrange("p (t h f) -> p t h f", t=4, h=NH),
                                    bc(oh_h[:, k, 4 * g:4 * g + 4, :], D), ALU.mult).then_inc(mk_done[2], 1)
                    dve.wait_ge(mk_done[2], j * 2 + g + 4)
                    if g == 0:
                        dve.wait_ge(vp_done, j * 6 + 4)
                    V.tensor_reduce(gx[:, k, 4 * g:4 * g + 4, :],
                                    mkf[:, k, 4 * g:4 * g + 4, :].rearrange("p t (h f) -> p t f h", h=NH),
                                    AX.X, ALU.add).then_inc(rd_done, 1)

                def step(j, i, k, ahead):
                    s = i * 4 + 2 * k
                    if ahead:
                        source_onehots(2, j + 1, i + k, 1 - k, 2, range(NC))
                    dve.wait_ge(g_in[2][k], (i + 1) * 16 * T)
                    edge_products(s, 0, gb[:, k, :, 0:D])
                    select_rows(j, k, 0)
                    low_parts(s, 0)
                    select_rows(j, k, 1)
                    dve.wait_ge(rd_done, j * 2 + 5)
                    edge_products(s + 1, 1, gx[:, k, :, :])
                    low_parts(s + 1, 1)
                    pair_onehots(1, j)

                source_onehots(2, 0, 0, 0, 2, range(NC))
                with dve.Fori(0, QUADS) as i:
                    for k in range(2):
                        step(i * 2 + k, i, k, True)
                step(PAIRS - 1, QUADS, 0, False)

            def convolution(p):
                w = p - 1
                dve.sem_inc(g_used[p], 2)
                dve.sem_inc(mk_done[p], 5)

                def step(j, i, k, ahead):
                    s = i * 4 + 2 * k
                    dve.wait_ge(mk_used[p], j + 1)
                    dve.wait_ge(hh_done[p], j + 1)
                    for g in range(4):
                        dve.wait_ge(gm_done[p], j * 4 + g + 6)
                        V.tensor_tensor(mk[:, k, 2 * g:2 * g + 2, :].rearrange("p t (h n) -> p t h n", h=NH),
                                        ps[:, 5 + g % 3, 0:2 * GW].rearrange("p (t h n) -> p t h n", t=2, h=NH),
                                        bc(oh_h[:, k, 2 * g:2 * g + 2, :], 3 * D), ALU.mult).then_inc(mk_done[p], 1)
                        if ahead:
                            source_onehots(p, j + 1, i + k, 1 - k, 4, [(0, 1), (2, 3), (4,), ()][g])
                    window_onehots(w, s)
                    window_onehots(w, s + 1)

                source_onehots(p, 0, 0, 0, 4, range(NC))
                with dve.Fori(0, QUADS) as i:
                    for k in range(2):
                        step(i * 2 + k, i, k, True)
                step(PAIRS - 1, QUADS, 0, False)

            for p in range(2, 5):
                if p == 2:
                    edge_network()
                else:
                    convolution(p)
                dve.wait_ge(s_accd, p + 2)
                if p == 2:
                    dve.wait_ge(s_vtab, 16)
                    for bk in range(NB // EBANK):
                        q = acc[:, bk * EBANK:(bk + 1) * EBANK, 0:3 * D]
                        av = ps[:, bk, 0:EBANK * EW].rearrange("p (q f) -> p q f", f=EW)
                        link(V.tensor_copy(q, av[:, :, 0:3 * D]))
                        link(V.tensor_tensor(q, q, av[:, :, 3 * D:6 * D], ALU.add))
                    link(V.tensor_tensor(acc[:, :, 0:3 * D], acc[:, :, 0:3 * D], bc(rcd[:, :], 3 * D), ALU.mult))
                    V.tensor_copy(acc[:, :, 3 * D:4 * D], x[:, :, :]).then_inc(s_nmi, 1)
                    res = node_product(4 * D)
                    link(V.tensor_tensor(t1[:, :, 0:D], res, over_nodes(par[:, B2, :], D), ALU.add))
                    link(V.tensor_tensor(t1[:, :, 0:D], t1[:, :, 0:D], bc(mask[:, :], D), ALU.mult))
                    batch_norm(t1[:, :, 0:D], GA, BE)
                    link(V.scalar_tensor_tensor(out=t2[:, :, 0:D], in0=t1[:, :, 0:D], scalar=0.01, in1=t1[:, :, 0:D],
                                                op0=ALU.mult, op1=ALU.max))
                    link(V.tensor_tensor(t2[:, :, 0:D], t2[:, :, 0:D], x[:, :, :], ALU.add))
                    link(V.tensor_tensor(x[:, :, :], t2[:, :, 0:D], x[:, :, :], ALU.add))
                    layer_norm(x[:, :, :])
                    dve.sem_inc(s_nmi, 1)
                    res = node_product(D)
                    dve.wait_ge(s_tab, 48)
                    scaled_table(res)
                    dve.sem_inc(s_node, 1)
                else:
                    for bk in range(-(-NB // ABANK)):
                        q, n = bk * ABANK, min(ABANK, NB - bk * ABANK)
                        link(V.tensor_reduce(t2[:, q:q + n, 0:D],
                                             ps[:, bk, 0:n * AW].rearrange("p (q g f) -> p q f g", g=NH, f=D),
                                             AX.X, ALU.add))
                    link(V.tensor_tensor(t2[:, :, 0:D], t2[:, :, 0:D], tab[:, :, 0:D], ALU.add))
                    link(V.tensor_tensor(t2[:, :, 0:D], t2[:, :, 0:D], bc(dinv[:, :], D), ALU.mult))
                    V.tensor_tensor(t1[:, :, 0:D], t2[:, :, 0:D],
                                    over_nodes(par[:, C1, :] if p == 3 else c2[:, :], D), ALU.add).then_inc(s_thi, 1)
                    dve.wait_ge(s_th, p - 2)
                    if p == 3:
                        dve.sem_inc(s_nmi, 1)
                        res = node_product(D)
                        dve.wait_ge(s_tab, 64)
                        scaled_table(res)
                        dve.sem_inc(s_node, 1)
                    else:
                        link(V.tensor_tensor(x[:, :, :], x[:, :, :], hh[:, :, :], ALU.add))
                        layer_norm(x[:, :, :])
                        dve.sem_inc(s_fin, 1)


def kernel(**inputs):
    import numpy as np
    import concourse.bacc as bacc
    from concourse import mybir as mb
    from concourse.bass_utils import run_bass_kernel_spmd as run

    g = {k: np.asarray(v) for k, v in inputs.items()}

    def pad_rows(v, n, fill=0):
        out = np.full((n,) + v.shape[1:], fill, v.dtype)
        out[:v.shape[0]] = v
        return out

    arrays = {
        "x": pad_rows(g["x"], NP_),
        "src": pad_rows(g["src"], EP, DUMP),
        "dst": pad_rows(g["dst"], EP, DUMP),
        "src_row": pad_rows(g["src"], EP, DUMP).reshape(NSUP, P, T).transpose(0, 2, 1).reshape(NSUP, SUP),
        "edge_attr_2": pad_rows(g["edge_attr_2"], EP),
        "edge_attr_3": pad_rows(g["edge_attr_3"], EP),
        "edge_attr_16": pad_rows(g["edge_attr_16"], EP),
        "eat": pad_rows(g["edge_attr_48"], EP).reshape(NSUP, P, T, EK).transpose(0, 3, 2, 1).reshape(NSUP, EK, SUP),
    }
    for l in range(2):
        w2 = np.concatenate([g[f"L1_gnn_fc{l}_w2"], g[f"L1_gnn_fc{l}_b2"][None]], axis=0)
        if l == 0:
            wa = w2[:, :D * D].reshape(EK + 1, D, D)
            wb = w2[:, D * D:].reshape(EK + 1, D, NV)
            w2 = np.concatenate([wb, wa], axis=2).reshape(EK + 1, D * MJ)
        arrays[f"w2_{l}"] = w2
        w1 = np.zeros((EK, P), np.float32)
        w1[:, :EK] = g[f"L1_gnn_fc{l}_w1"]
        arrays[f"w1_{l}"] = w1
        arrays[f"b1_{l}"] = g[f"L1_gnn_fc{l}_b1"]
    arrays["w_enet"] = g["L2_gnn_W_enet"].reshape(2 * D, D)
    arrays["b_enet"] = g["L2_gnn_b_enet"].reshape(D, D)
    arrays["w_root"] = g["L2_gnn_W_root"]
    arrays["gw1"] = g["L3_gnn_W1"]
    arrays["gw2"] = g["L3_gnn_W2"]
    for short, full in (("gs0", "L1_gnn_bn0_gs"), ("bs0", "L1_gnn_bn0_bs"), ("gv0", "L1_gnn_bn0_gv"),
                        ("gs1", "L1_gnn_bn1_gs"), ("bs1", "L1_gnn_bn1_bs"), ("bias", "L2_gnn_bias"),
                        ("gamma", "L2_gnn_gamma"), ("beta", "L2_gnn_beta"), ("gb1", "L3_gnn_b1"), ("gb2", "L3_gnn_b2")):
        arrays[short] = g[full]
    nc = bacc.Bacc("TRN2", target_bir_lowering=False, num_devices=1)
    feeds, aps = {}, {}
    for name, v in arrays.items():
        v = np.ascontiguousarray(v)
        feeds[f"in_{name}"] = v
        aps[name] = nc.dram_tensor(f"in_{name}", v.shape, mb.dt.from_np(v.dtype), kind="ExternalInput").ap()
    aps["out"] = nc.dram_tensor("out_x", (N, D), mb.dt.float32, kind="ExternalOutput").ap()
    build(nc, aps)
    r = run(nc, [feeds], core_ids=[0])
    return r.results[0]["out_x"]
```
